# Optimizing a Trainium2 kernel written in Bass

```python
import numpy as np
import jax
import jax.numpy as jnp

def _softmax(x, axis=-1):
    return jax.nn.softmax(x, axis=axis)

def _gelu(x):
    return jax.nn.gelu(x, approximate=True)

def _silu(x):
    return jax.nn.silu(x)

def _sigmoid(x):
    return jax.nn.sigmoid(x)

def _layernorm(x, axis=-1, eps=1e-05):
    m = jnp.mean(x, axis=axis, keepdims=True)
    v = jnp.var(x, axis=axis, keepdims=True)
    return (x - m) / jnp.sqrt(v + eps)

def _scatter_add(tgt, idx, src, axis=0):
    return tgt.at[idx].add(src)

def _segment_sum(src, seg, n):
    return jax.ops.segment_sum(src, seg, n)
kernel_name = 'mk_dlrm_tower_d1_rec_r8_5e6451'

def setup_inputs(seed: int=0):
    np.random.seed(seed)
    _w = jnp.asarray

    def _rec_inputs():
        import jax
        import jax.numpy as jnp
        _tk = jax.random.key(seed)
        ids = jnp.stack([jax.random.randint(jax.random.fold_in(_tk, 200 + f), (2048,), 0, v, jnp.int32) for f, v in enumerate([1000, 12500, 12500, 125000, 1000, 12500, 1250, 1000, 12500, 1000, 1250, 1250, 12500, 12500, 1250, 12500, 1000, 1000, 12500, 1250, 1000, 1000, 1250, 1250, 1250, 1000])], axis=1)
        tbl_0 = 0.05 * jax.random.normal(jax.random.fold_in(_tk, 500 + 0), (1000, 128), jnp.float32)
        tbl_1 = 0.05 * jax.random.normal(jax.random.fold_in(_tk, 500 + 1), (12500, 128), jnp.float32)
        tbl_2 = 0.05 * jax.random.normal(jax.random.fold_in(_tk, 500 + 2), (12500, 128), jnp.float32)
        tbl_3 = 0.05 * jax.random.normal(jax.random.fold_in(_tk, 500 + 3), (125000, 128), jnp.float32)
        tbl_4 = 0.05 * jax.random.normal(jax.random.fold_in(_tk, 500 + 4), (1000, 128), jnp.float32)
        tbl_5 = 0.05 * jax.random.normal(jax.random.fold_in(_tk, 500 + 5), (12500, 128), jnp.float32)
        tbl_6 = 0.05 * jax.random.normal(jax.random.fold_in(_tk, 500 + 6), (1250, 128), jnp.float32)
        tbl_7 = 0.05 * jax.random.normal(jax.random.fold_in(_tk, 500 + 7), (1000, 128), jnp.float32)
        tbl_8 = 0.05 * jax.random.normal(jax.random.fold_in(_tk, 500 + 8), (12500, 128), jnp.float32)
        tbl_9 = 0.05 * jax.random.normal(jax.random.fold_in(_tk, 500 + 9), (1000, 128), jnp.float32)
        tbl_10 = 0.05 * jax.random.normal(jax.random.fold_in(_tk, 500 + 10), (1250, 128), jnp.float32)
        tbl_11 = 0.05 * jax.random.normal(jax.random.fold_in(_tk, 500 + 11), (1250, 128), jnp.float32)
        tbl_12 = 0.05 * jax.random.normal(jax.random.fold_in(_tk, 500 + 12), (12500, 128), jnp.float32)
        tbl_13 = 0.05 * jax.random.normal(jax.random.fold_in(_tk, 500 + 13), (12500, 128), jnp.float32)
        tbl_14 = 0.05 * jax.random.normal(jax.random.fold_in(_tk, 500 + 14), (1250, 128), jnp.float32)
        tbl_15 = 0.05 * jax.random.normal(jax.random.fold_in(_tk, 500 + 15), (12500, 128), jnp.float32)
        tbl_16 = 0.05 * jax.random.normal(jax.random.fold_in(_tk, 500 + 16), (1000, 128), jnp.float32)
        tbl_17 = 0.05 * jax.random.normal(jax.random.fold_in(_tk, 500 + 17), (1000, 128), jnp.float32)
        tbl_18 = 0.05 * jax.random.normal(jax.random.fold_in(_tk, 500 + 18), (12500, 128), jnp.float32)
        tbl_19 = 0.05 * jax.random.normal(jax.random.fold_in(_tk, 500 + 19), (1250, 128), jnp.float32)
        tbl_20 = 0.05 * jax.random.normal(jax.random.fold_in(_tk, 500 + 20), (1000, 128), jnp.float32)
        tbl_21 = 0.05 * jax.random.normal(jax.random.fold_in(_tk, 500 + 21), (1000, 128), jnp.float32)
        tbl_22 = 0.05 * jax.random.normal(jax.random.fold_in(_tk, 500 + 22), (1250, 128), jnp.float32)
        tbl_23 = 0.05 * jax.random.normal(jax.random.fold_in(_tk, 500 + 23), (1250, 128), jnp.float32)
        tbl_24 = 0.05 * jax.random.normal(jax.random.fold_in(_tk, 500 + 24), (1250, 128), jnp.float32)
        tbl_25 = 0.05 * jax.random.normal(jax.random.fold_in(_tk, 500 + 25), (1000, 128), jnp.float32)
        _rk = jax.random.fold_in(_tk, 7)
        r_bottom_output = -0.000520686 + 1.00062 * jax.random.normal(jax.random.fold_in(_rk, 101), (2048, 128), jnp.float32)
        W_top1 = 0.0456912 * jax.random.normal(jax.random.fold_in(_tk, 801), (479, 512), jnp.float32)
        W_top2 = 0.0441942 * jax.random.normal(jax.random.fold_in(_tk, 802), (512, 256), jnp.float32)
        W_top3 = 0.0625 * jax.random.normal(jax.random.fold_in(_tk, 803), (256, 1), jnp.float32)
        b_top1 = jnp.zeros((512,), jnp.float32)
        b_top2 = jnp.zeros((256,), jnp.float32)
        return (r_bottom_output, ids, tbl_0, tbl_1, tbl_2, tbl_3, tbl_4, tbl_5, tbl_6, tbl_7, tbl_8, tbl_9, tbl_10, tbl_11, tbl_12, tbl_13, tbl_14, tbl_15, tbl_16, tbl_17, tbl_18, tbl_19, tbl_20, tbl_21, tbl_22, tbl_23, tbl_24, tbl_25, W_top1, b_top1, W_top2, b_top2, W_top3)
    r_bottom_output, ids, tbl_0, tbl_1, tbl_2, tbl_3, tbl_4, tbl_5, tbl_6, tbl_7, tbl_8, tbl_9, tbl_10, tbl_11, tbl_12, tbl_13, tbl_14, tbl_15, tbl_16, tbl_17, tbl_18, tbl_19, tbl_20, tbl_21, tbl_22, tbl_23, tbl_24, tbl_25, W_top1, b_top1, W_top2, b_top2, W_top3 = _rec_inputs()

    def _L0_rec_setup():
        import jax, jax.numpy as jnp
        import numpy as np
        NUM_FEATURES = 27
        _TRIU_I, _TRIU_J = np.triu_indices(NUM_FEATURES, k=1)
        key = jax.random.key(seed)
        k1, k2 = jax.random.split(key)
        bottom_output = jax.random.normal(k1, (2048, 128), dtype=jnp.float32)
        embeddings = jax.random.normal(k2, (2048, 26, 128), dtype=jnp.float32)
        return {'bottom_output': bottom_output, 'embeddings': embeddings}
    _L0_rec_all = _L0_rec_setup()
    _L0_rec_in = {k: v for k, v in _L0_rec_all.items() if k in ()}
    del _L0_rec_all
    return {'r_bottom_output': r_bottom_output, 'ids': ids, 'tbl_0': tbl_0, 'tbl_1': tbl_1, 'tbl_2': tbl_2, 'tbl_3': tbl_3, 'tbl_4': tbl_4, 'tbl_5': tbl_5, 'tbl_6': tbl_6, 'tbl_7': tbl_7, 'tbl_8': tbl_8, 'tbl_9': tbl_9, 'tbl_10': tbl_10, 'tbl_11': tbl_11, 'tbl_12': tbl_12, 'tbl_13': tbl_13, 'tbl_14': tbl_14, 'tbl_15': tbl_15, 'tbl_16': tbl_16, 'tbl_17': tbl_17, 'tbl_18': tbl_18, 'tbl_19': tbl_19, 'tbl_20': tbl_20, 'tbl_21': tbl_21, 'tbl_22': tbl_22, 'tbl_23': tbl_23, 'tbl_24': tbl_24, 'tbl_25': tbl_25, 'W_top1': W_top1, 'b_top1': b_top1, 'W_top2': W_top2, 'b_top2': b_top2, 'W_top3': W_top3}

def reference(r_bottom_output, ids, tbl_0, tbl_1, tbl_2, tbl_3, tbl_4, tbl_5, tbl_6, tbl_7, tbl_8, tbl_9, tbl_10, tbl_11, tbl_12, tbl_13, tbl_14, tbl_15, tbl_16, tbl_17, tbl_18, tbl_19, tbl_20, tbl_21, tbl_22, tbl_23, tbl_24, tbl_25, W_top1, b_top1, W_top2, b_top2, W_top3):
    import jax
    import jax.numpy as jnp

    def _L0_rec_ref(bottom_output, embeddings):
        import jax, jax.numpy as jnp
        import numpy as np
        NUM_FEATURES = 27
        _TRIU_I, _TRIU_J = np.triu_indices(NUM_FEATURES, k=1)
        all_emb = jnp.concatenate([bottom_output[:, None, :], embeddings], axis=1)
        gram = jnp.einsum('bfd,bgd->bfg', all_emb, all_emb)
        return gram[:, _TRIU_I, _TRIU_J]
    e = jnp.stack([tbl_0[ids[:, 0]], tbl_1[ids[:, 1]], tbl_2[ids[:, 2]], tbl_3[ids[:, 3]], tbl_4[ids[:, 4]], tbl_5[ids[:, 5]], tbl_6[ids[:, 6]], tbl_7[ids[:, 7]], tbl_8[ids[:, 8]], tbl_9[ids[:, 9]], tbl_10[ids[:, 10]], tbl_11[ids[:, 11]], tbl_12[ids[:, 12]], tbl_13[ids[:, 13]], tbl_14[ids[:, 14]], tbl_15[ids[:, 15]], tbl_16[ids[:, 16]], tbl_17[ids[:, 17]], tbl_18[ids[:, 18]], tbl_19[ids[:, 19]], tbl_20[ids[:, 20]], tbl_21[ids[:, 21]], tbl_22[ids[:, 22]], tbl_23[ids[:, 23]], tbl_24[ids[:, 24]], tbl_25[ids[:, 25]]], axis=1)
    z = _L0_rec_ref(r_bottom_output, e)
    z = z.reshape(z.shape[0], -1)
    h = jnp.concatenate([z, r_bottom_output], axis=1)
    h = jnp.maximum(h @ W_top1 + b_top1, 0.0)
    h = jnp.maximum(h @ W_top2 + b_top2, 0.0)
    y = h @ W_top3
    return y

_drawn_inputs = setup_inputs


def setup_inputs(seed=0):
    import zlib

    import numpy as np

    out = dict(_drawn_inputs(seed))
    spreads = {'b_top1': (0.0, 0.1), 'b_top2': (0.0, 0.1)}
    factors = {}
    for name, (base, spread) in spreads.items():
        noise = np.random.default_rng([zlib.crc32(name.encode()), seed]).standard_normal(out[name].shape)
        drawn = base * np.exp(spread * noise) if base else spread * noise
        out[name] = jnp.asarray(drawn.astype(out[name].dtype))
    for name, factor in factors.items():
        out[name] = (out[name] * factor).astype(out[name].dtype)
    return out
```

```python
import concourse.bass as bass
from concourse import mybir
from contextlib import ExitStack

def dlrm_tower(nc, bottom, ids, ids_small, tables, small, w1, b1, w2, b2, w3, out):
    fp32 = mybir.dt.float32
    i32 = mybir.dt.int32
    i16 = mybir.dt.int16
    u16 = mybir.dt.uint16
    bf16 = mybir.dt.bfloat16
    ALU = mybir.AluOpType
    ACT = mybir.ActivationFunctionType

    B, D = bottom.shape
    NT = len(tables)
    NS = len(small)
    F = 1 + NT + NS
    P = 128
    TILES = B // P
    PAIRS = TILES // 2
    GF = 4
    GROUPS = (1 + NT + GF - 1) // GF
    FP = 32
    H = F // 2
    W = F + H
    Q = 32
    KT = 3
    KP = F * H // KT
    N1, N2 = w1.shape[1], w2.shape[1]
    C1, C2 = N1 // P, N2 // P
    NP = 2 * P
    PARTS = 3
    SC = 8
    SP = small[0].shape[0] // SC
    SU = (NS + 1) // 2
    SG = P // FP
    UG = 8
    UNITS = Q // UG
    RB = 4

    A, V = "scalar", "vector"
    GROUP_BY = [V, A, A, V, A, A, V][:GROUPS]
    SMALL_BY = [A, V, A, V][:SU]
    UNIT_BY = [A, V] * (UNITS // 2)
    STEP = [(("group", 1, g), 0) for g in range(GROUPS)]
    STEP += [(("small", 0), 1), (("z", 0), 0)]
    STEP += [(("group", 0, g), 1) for g in range(GROUPS)]
    STEP += [(("small", u), 1) for u in range(1, SU)]
    STEP += [(("z", 1), 0), (("h1", 0), 0), (("h1", 1), 0), (("h2", 0), 0), (("h2", 1), 0), (("y", 0), 0)]
    NAMES = [name for name, _ in STEP]
    BANK = {name: n % RB for n, name in enumerate(NAMES)}
    BY = {("z", 0): V, ("z", 1): V, ("h1", 0): A, ("h1", 1): A, ("h2", 0): A, ("h2", 1): A, ("y", 0): V}
    BY |= {("small", u): SMALL_BY[u] for u in range(SU)}
    BY |= {("group", k, g): GROUP_BY[g] for k in range(2) for g in range(GROUPS)}
    AHEAD = ("z", "h1", "h2", "y")
    assert len(GROUP_BY) == GROUPS and F <= FP and C1 == 4 and C2 == 2 and 2 * NP == 512

    ctx = ExitStack()
    with ctx:
        def sb(name, shape, dt):
            return ctx.enter_context(nc.sbuf_tensor(name, shape, dt))

        def sem(name):
            return ctx.enter_context(nc.semaphore(name))

        ident = sb("ident", [P, P], fp32)
        ident_b = sb("ident_b", [P, P], bf16)
        idx = sb("idx", [P, 2, NT], i32)
        e = sb("e", [P, 2, 1 + NT, D], fp32)
        eT = sb("eT", [P, 2, P, FP], fp32)
        rT = sb("rT", [P, NP], fp32)
        parts = sb("parts", [SP, NS, PARTS, SC, D], bf16)
        row_of = sb("row_of", [SP, SC], fp32)
        row_of_i = sb("row_of_i", [SP, SC], i32)
        ids_b = sb("ids_b", [P, NS, NP], i32)
        ids_h = sb("ids_h", [P, NS, NP], i16)
        onehot = sb("onehot", [SP, SC, NS, NP], bf16)
        gr = sb("gr", [P, 2, Q, F], fp32)
        z = sb("z", [P, 2, Q, W], fp32)
        zc = sb("zc", [P, 2, F * H], fp32)
        zT = sb("zT", [KP, KT, NP], fp32)
        w1z = sb("w1z", [KP, KT, N1], fp32)
        w1r = sb("w1r", [D, N1], fp32)
        w2s = sb("w2s", [P, C1, N2], fp32)
        w3s = sb("w3s", [P, C2], fp32)
        b1s = sb("b1s", [P, C1], fp32)
        b2s = sb("b2s", [P, C2], fp32)
        h1 = sb("h1", [P, C1, NP], fp32)
        h2 = sb("h2", [P, C2, NP], fp32)
        y = sb("y", [1, B], fp32)

        ring = [ctx.enter_context(nc.psum_tensor(f"ring{i}", [P, 512], fp32)) for i in range(RB)]
        gram = [ctx.enter_context(nc.psum_tensor(f"gram{i}", [P, 2, 512], fp32)) for i in range(2)]

        s_ident0 = sem("ident_cleared")
        s_ident = sem("ident_ready")
        s_ident_b = sem("ident_b_ready")
        s_w = sem("weights_loaded")
        s_idx = [sem(f"idx_loaded{k}") for k in range(2)]
        s_r = [sem(f"bottom_loaded{k}") for k in range(2)]
        s_g = [[sem(f"gathered{k}_{g}") for g in range(GROUPS)] for k in range(2)]
        s_tr = sem("group_transposed")
        s_copied = {key: sem(f"{key[0]}_copied_by_{key[1]}") for key in sorted({(n[0], BY[n]) for n in NAMES})}
        s_gram = sem("gram_done")
        s_z = sem("z_ready")
        s_iota = sem("rows_numbered")
        s_row_of = sem("row_of_ready")
        s_ids_b = sem("small_ids_loaded")
        s_ids_h = sem("small_ids_narrowed")
        s_onehot = sem("onehot_ready")
        s_tab = [sem(f"small_table_loaded{j}") for j in range(NS)]
        s_split = {A: sem("split_by_scalar"), V: sem("split_by_vector")}
        s_pad = sem("eT_padding_cleared")
        s_small = sem("small_summed")
        s_unit = {A: sem("unit_copied_by_scalar"), V: sem("unit_copied_by_vector")}
        s_zc = sem("pairs_packed")
        s_zp = sem("z_transposed")
        s_h1p = sem("h1_summed")
        s_h2p = sem("h2_summed")
        s_yp = sem("y_summed")
        s_out = sem("out_stored")
        s_tile_turn = sem("tile_turn")
        s_group_turn = sem("group_turn")

        def slots(g):
            return range(GF * g, min(GF * (g + 1), 1 + NT))

        def bank(name):
            return ring[BANK[name]]

        def key(name):
            return name[0], BY[name]

        def copied(i, name):
            same = sorted(n for n in NAMES if key(n) == key(name))
            return i * len(same) + (same.index(name) + 1 + len(same) * (name[0] in AHEAD))

        def wait_copied(engine, i, *names):
            for k in sorted({key(n) for n in names}):
                engine.wait_ge(s_copied[k], copied(i, max(n for n in names if key(n) == k)))

        def z_pairs(k):
            flat = z[:, k, :, :].rearrange("p f w -> p (f w)")
            skew = flat[:, 0:(Q * W) // (W + 1) * (W + 1)].rearrange("p (f w) -> p f w", w=W + 1)
            return skew[:, 0:F, 1:H + 1]

        def group_copy(copy, k, g):
            n = 2 * len(slots(g))
            src = bank(("group", k, g))[:, :].bitcast(u16)[:, 0:n * P].rearrange("p (f b) -> p b f", f=n)
            return copy(eT16[:, k, :, 2 * GF * g:2 * GF * g + n], src)

        def small_copy(copy, u):
            n = min(2, NS - 2 * u)
            f = 1 + NT + 2 * u
            src = bank(("small", u))[:, 0:n * NP].rearrange("p (f b) -> p b f", f=n)
            return copy(eT[:].rearrange("p k b f -> p (k b) f")[:, :, f:f + n], src)

        eT16 = eT[:].rearrange("p k b f -> p (k b f)").bitcast(u16).rearrange("p (k b f) -> p k b f", k=2, b=P)
        e16 = e[:].rearrange("p k s d -> p (k s d)").bitcast(bf16).rearrange("p (k s d h) -> p k s h d", k=2, d=D, h=2)

        ids_t = ids.rearrange("(t p) f -> t p f", p=P)
        bottom_t = bottom.rearrange("(t p) d -> t p d", p=P)
        whole = eT[:].rearrange("p k b f -> p (k b f)")[0:SP, :].rearrange("p (j c d) -> p j c d", c=SC, d=D)

        block = ctx.enter_context(nc.Block())

        @block.sync
        def _(sp):
            def load_tile(t, k):
                sp.dma_start(idx[:, k, :], ids_t[t]).then_inc(s_idx[k], 16)
                sp.dma_start(e[:, k, 0, :], bottom_t[t]).then_inc(s_r[k], 16)

            def load_small_ids(i):
                src = ids_small[:, bass.ds(i * NP, NP)].rearrange("(o j) b -> o j b", o=1)
                sp.dma_start(ids_b[:], src.to_broadcast([P, NS, NP])).then_inc(s_ids_b, 16)

            load_tile(0, 0)
            load_tile(1, 1)
            load_small_ids(0)
            for j in range(NS):
                sp.dma_start(whole[:, j], small[j].rearrange("(p c) d -> p c d", c=SC)).then_inc(s_tab[j], 16)
            sp.dma_start(w1z[:], w1[0:KT * KP, :].rearrange("(m p) n -> p m n", p=KP)).then_inc(s_w, 16)
            sp.dma_start(w1r[:], w1[KT * KP:KT * KP + D, :]).then_inc(s_w, 16)
            sp.dma_start(w2s[:], w2.rearrange("(c p) n -> p c n", p=P)).then_inc(s_w, 16)
            with nc.allow_non_contiguous_dma(reason="small vectors"):
                sp.dma_start(w3s[:], w3.rearrange("(c p) o -> p (c o)", p=P)).then_inc(s_w, 16)
                sp.dma_start(b1s[:], b1.rearrange("(c p) -> p c", p=P)).then_inc(s_w, 16)
                sp.dma_start(b2s[:], b2.rearrange("(c p) -> p c", p=P)).then_inc(s_w, 16)
            sp.wait_ge(s_ids_h, 1)
            load_small_ids(1)
            with sp.Fori(1, PAIRS) as i:
                for k in range(2):
                    sp.wait_ge(s_tr, (i - 1) * (2 * GROUPS) + (k + 1) * GROUPS)
                    sp.sem_inc(s_tile_turn, 1)
                    load_tile(i * 2 + k, k)
                    if k == 0:
                        sp.wait_ge(s_ids_h, i + 1)
                        sp.sem_inc(s_tile_turn, 1)
                        load_small_ids(i + 1)
            wait_copied(sp, PAIRS - 1, ("y", 0))
            sp.dma_start(out.rearrange("b o -> o b"), y[:]).then_inc(s_out, 16)
            sp.wait_ge(s_out, 16)

        @block.gpsimd
        def _(pool):
            nc.gpsimd.memset(ident[:], 0.0).then_inc(s_ident0, 1)
            pool.wait_ge(s_ident0, 1)
            nc.gpsimd.affine_select(out=ident[:], in_=ident[:], compare_op=ALU.not_equal, fill=1.0,
                                    base=0, pattern=[[-1, P]], channel_multiplier=1).then_inc(s_ident, 1)
            nc.gpsimd.iota(row_of_i[:], pattern=[[1, SC]], base=0, channel_multiplier=SC).then_inc(s_iota, 1)

            def gathers(i, k, first):
                pool.wait_ge(s_idx[k], i * 16 + 16)
                pool.sem_inc(s_group_turn, 1)
                for g in range(GROUPS):
                    if not first:
                        pool.wait_ge(s_tr, (i - 1) * (2 * GROUPS) + (k * GROUPS + g + 1))
                        pool.sem_inc(s_group_turn, 1)
                    for s in slots(g):
                        if s:
                            nc.gpsimd.indirect_dma_start(
                                out=e[:, k, s, :], out_offset=None, in_=tables[s - 1],
                                in_offset=bass.IndirectOffsetOnAxis(ap=idx[:, k, s - 1:s], axis=0),
                            ).then_inc(s_g[k][g], 16)

            for k in range(2):
                gathers(0, k, True)
            with pool.Fori(1, PAIRS) as i:
                for k in range(2):
                    gathers(i, k, False)

        @block.tensor
        def _(pe):
            def take(i, name):
                n = NAMES.index(name)
                last = isinstance(i, int) and i == PAIRS - 1 and not STEP[n][1]
                same = [m for m in range(len(STEP)) if BANK[NAMES[m]] == BANK[name] and not (last and STEP[m][1])]
                before = [m for m in same if m < n]
                m = (before or same)[-1]
                step = i - STEP[n][1] if before else i - STEP[n][1] - 1
                value = copied(step + STEP[m][1], NAMES[m])
                if not isinstance(value, int) or value > 0:
                    pe.wait_ge(s_copied[key(NAMES[m])], value)
                return bank(name)

            def small_tables(i, uses):
                pe.wait_ge(s_onehot, i + 1)
                for u in uses:
                    dst = take(i, ("small", u))
                    for n in range(min(2, NS - 2 * u)):
                        j = 2 * u + n
                        for part in range(PARTS):
                            for c in range(SC):
                                last = nc.tensor.matmul(dst[:, n * NP:(n + 1) * NP], parts[:, j, part, c, :],
                                                        onehot[:, c, j, :], start=part == 0 and c == 0,
                                                        stop=part == PARTS - 1 and c == SC - 1)
                    last.then_inc(s_small, 1)

            def transposes(i, k):
                pe.wait_ge(s_r[k], i * 16 + 16)
                for g in range(GROUPS):
                    pe.wait_ge(s_g[k][g], (i + 1) * (16 * len([s for s in slots(g) if s])))
                    dst = take(i, ("group", k, g))
                    for n, s in enumerate(slots(g)):
                        for h in range(2):
                            at = (2 * n + h) * P
                            last = nc.tensor.transpose(dst[:, :].bitcast(bf16)[:, at:at + P], e16[:, k, s, h, :],
                                                       ident_b[:])
                    last.then_inc(s_tr, 1)

            def grams(i, k):
                wait_copied(pe, i, *[("small", u) for u in range(SU)], *[("group", k, g) for g in range(GROUPS)])
                for u in range(UNITS):
                    pe.wait_ge(s_unit[UNIT_BY[u]], i * UNITS + (k * UNITS // 2 + u // 2 + 1))
                    for n in range(UG):
                        v = eT[:, k, SG * (UG * u + n):SG * (UG * u + n + 1), :]
                        per = UG // 2
                        col = n % per * SG * F
                        last = nc.tensor.matmul(gram[u % 2][:, n // per, col:col + SG * F],
                                                v.rearrange("p s f -> p (s f)"), v[:, :, 0:F],
                                                start=True, stop=True, skip_group_check=True)
                    last.then_inc(s_gram, 1)

            def z_transposes(i, k):
                pe.wait_ge(s_zc, i * 2 + (k + 1))
                dst = take(i, ("z", k))
                for m in range(KT):
                    last = nc.tensor.transpose(dst[0:KP, m * P:(m + 1) * P], zc[:, k, m * KP:(m + 1) * KP], ident[:])
                last.then_inc(s_zp, 1)

            def mlp(i):
                wait_copied(pe, i, ("z", 0), ("z", 1))
                for u in range(2):
                    dst = take(i, ("h1", u))
                    for v in range(2):
                        c = 2 * u + v
                        o = dst[:, v * NP:(v + 1) * NP]
                        for m in range(KT):
                            nc.tensor.matmul(o, w1z[:, m, c * P:(c + 1) * P], zT[:, m, :],
                                             start=m == 0, stop=False)
                        last = nc.tensor.matmul(o, w1r[:, c * P:(c + 1) * P], rT[:], start=False, stop=True)
                    last.then_inc(s_h1p, 1)
                for v in range(C2):
                    dst = take(i, ("h2", v))
                    for c in range(C1):
                        if v == 0 and c % 2 == 0:
                            wait_copied(pe, i, ("h1", c // 2))
                        last = nc.tensor.matmul(dst[:, 0:NP], w2s[:, c, v * P:(v + 1) * P],
                                                h1[:, c, :], start=c == 0, stop=c == C1 - 1)
                    last.then_inc(s_h2p, 1)
                dst = take(i, ("y", 0))
                for c in range(C2):
                    wait_copied(pe, i, ("h2", c))
                    last = nc.tensor.matmul(dst[0:1, 0:NP], w3s[:, c:c + 1], h2[:, c, :],
                                            start=c == 0, stop=c == C2 - 1)
                last.then_inc(s_yp, 1)

            pe.wait_ge(s_ident, 1)
            pe.wait_ge(s_ident_b, 1)
            pe.wait_ge(s_w, 16 * 6)
            pe.wait_ge(s_split[A], 2 * NS)
            pe.wait_ge(s_split[V], 2 * NS)
            pe.wait_ge(s_pad, 1)
            small_tables(0, [0])
            transposes(0, 0)
            small_tables(0, range(1, SU))
            grams(0, 0)
            with pe.Fori(0, PAIRS - 1) as i:
                transposes(i, 1)
                small_tables(i + 1, [0])
                grams(i, 1)
                z_transposes(i, 0)
                transposes(i + 1, 0)
                small_tables(i + 1, range(1, SU))
                z_transposes(i, 1)
                grams(i + 1, 0)
                mlp(i)
            transposes(PAIRS - 1, 1)
            grams(PAIRS - 1, 1)
            z_transposes(PAIRS - 1, 0)
            z_transposes(PAIRS - 1, 1)
            mlp(PAIRS - 1)


        def copy_small(engine, copy, by, i, uses, first=False):
            for u in uses:
                if SMALL_BY[u] == by:
                    if not first:
                        engine.wait_ge(s_gram, i * (2 * UNITS))
                    engine.wait_ge(s_small, i * SU + (u + 1))
                    small_copy(copy, u).then_inc(s_copied["small", by], 1)

        def copy_groups(engine, copy, by, i, k):
            for g in range(GROUPS):
                if GROUP_BY[g] == by:
                    if g == 0:
                        wait_copied(engine, i - 1, ("z", k))
                    engine.wait_ge(s_tr, i * (2 * GROUPS) + (k * GROUPS + g + 1))
                    group_copy(copy, k, g).then_inc(s_copied["group", by], 1)

        def copy_units(engine, copy, by, i, k):
            engine.wait_ge(s_z, i * 2 + (k + 1))
            for u in range(UNITS):
                if UNIT_BY[u] == by:
                    engine.wait_ge(s_gram, i * (2 * UNITS) + (k * UNITS + u + 1))
                    for s in range(SG):
                        rows = slice(FP * s, FP * (s + 1))
                        src = gram[u % 2][rows, :, 0:UG // 2 * SG * F].rearrange("p h (g w) -> p h g w", w=SG * F)
                        dst = gr[rows, k, UG * u:UG * (u + 1), :].rearrange("p (h g) f -> p h g f", h=2)
                        last = copy(dst, src[:, :, :, s * F:(s + 1) * F])
                    last.then_inc(s_unit[by], 1)

        @block.scalar
        def _(act):
            for j in range(NS):
                act.wait_ge(s_tab[j], 16)
                nc.scalar.copy(parts[:, j, 0], whole[:, j]).then_inc(s_split[A], 1)
            for j in range(NS):
                act.wait_ge(s_split[V], j + 1)
                nc.scalar.copy(parts[:, j, 1], whole[:, j]).then_inc(s_split[A], 1)
            act.wait_ge(s_w, 16 * 6)
            act.sem_inc(s_copied["h1", A], 2)
            act.sem_inc(s_copied["h2", A], 2)
            act.sem_inc(s_unit[A], 1)

            def pack(i, k):
                act.wait_ge(s_z, i * 2 + (k + 3))
                nc.scalar.copy(zc[:, k, :].rearrange("p (f o) -> p f o", f=F), z_pairs(k)).then_inc(s_zc, 1)

            def hidden(i):
                for u in range(2):
                    act.wait_ge(s_h1p, i * 2 + (u + 1))
                    for v in range(2):
                        c = 2 * u + v
                        last = nc.scalar.activation(h1[:, c, :], bank(("h1", u))[:, v * NP:(v + 1) * NP], ACT.Relu,
                                                    bias=b1s[:, c:c + 1])
                    last.then_inc(s_copied["h1", A], 1)
                for v in range(C2):
                    act.wait_ge(s_h2p, i * C2 + (v + 1))
                    nc.scalar.activation(h2[:, v, :], bank(("h2", v))[:, 0:NP], ACT.Relu,
                                         bias=b2s[:, v:v + 1]).then_inc(s_copied["h2", A], 1)

            copy = nc.scalar.copy
            copy_small(act, copy, A, 0, [0], first=True)
            copy_groups(act, copy, A, 0, 0)
            copy_small(act, copy, A, 0, range(1, SU), first=True)
            copy_units(act, copy, A, 0, 0)
            with act.Fori(0, PAIRS - 1) as i:
                copy_groups(act, copy, A, i, 1)
                pack(i, 0)
                copy_units(act, copy, A, i, 1)
                copy_small(act, copy, A, i + 1, [0])
                copy_groups(act, copy, A, i + 1, 0)
                pack(i, 1)
                copy_small(act, copy, A, i + 1, range(1, SU))
                copy_units(act, copy, A, i + 1, 0)
                hidden(i)
            copy_groups(act, copy, A, PAIRS - 1, 1)
            pack(PAIRS - 1, 0)
            copy_units(act, copy, A, PAIRS - 1, 1)
            pack(PAIRS - 1, 1)
            hidden(PAIRS - 1)

        @block.vector
        def _(dve):
            copy = nc.vector.tensor_copy
            dve.sem_inc(s_z, 2)
            dve.sem_inc(s_copied["z", V], 2)
            dve.sem_inc(s_copied["y", V], 1)
            dve.sem_inc(s_unit[V], 1)

            def one_hot(i):
                dve.wait_ge(s_ids_b, i * 16 + 16)
                copy(ids_h[:], ids_b[:]).then_inc(s_ids_h, 1)
                dve.wait_ge(s_ids_h, i + 1)
                for c in range(SC):
                    last = nc.vector.tensor_scalar(onehot[:, c], ids_h[0:SP], row_of[:, c:c + 1], None, ALU.is_equal)
                last.then_inc(s_onehot, 1)

            dve.wait_ge(s_ident, 1)
            copy(ident_b[:], ident[:]).then_inc(s_ident_b, 1)
            dve.wait_ge(s_iota, 1)
            copy(row_of[:], row_of_i[:]).then_inc(s_row_of, 1)
            dve.wait_ge(s_row_of, 1)
            one_hot(0)
            for part in range(2):
                for j in range(NS):
                    dve.wait_ge(s_split[A], part * NS + j + 1)
                    dst = parts[:, j, 2] if part else whole[:, j]
                    nc.vector.tensor_tensor(dst, whole[:, j], parts[:, j, part], ALU.subtract).then_inc(s_split[V], 1)
            dve.wait_ge(s_split[V], 2 * NS)
            nc.vector.memset(eT[:, :, :, F:FP], 0.0).then_inc(s_pad, 1)

            def gram_rows(i, k):
                for by in (A, V):
                    dve.wait_ge(s_unit[by], i * UNITS + ((k + 1) * UNITS // 2 + 1))
                nc.vector.transpose(z[:, k, :, 0:F].rearrange("p f g -> p g f"),
                                    gr[:, k].rearrange("p q g -> p g q"))
                nc.vector.transpose(z[:, k, :, F:W].rearrange("p f g -> p g f"),
                                    gr[:, k, :, 0:H].rearrange("p q g -> p g q")).then_inc(s_z, 1)

            def copy_pairs(i, k):
                dve.wait_ge(s_zp, i * 2 + (k + 1))
                src = bank(("z", k))[0:KP, 0:KT * P].rearrange("p (m s q) -> p m q s", m=KT, s=SG)
                dst = zT[:, :, k * P:(k + 1) * P].rearrange("p m (q s) -> p m q s", s=SG)
                copy(rT[:, k * P:(k + 1) * P], eT[:, k, :, 0])
                copy(dst, src).then_inc(s_copied["z", V], 1)

            def copy_y(i):
                dve.wait_ge(s_yp, i + 1)
                copy(y[:, bass.ds(i * NP, NP)], bank(("y", 0))[0:1, 0:NP]).then_inc(s_copied["y", V], 1)

            def next_one_hot(i):
                dve.wait_ge(s_small, i * SU + SU)
                one_hot(i + 1)

            copy_small(dve, copy, V, 0, [0], first=True)
            copy_groups(dve, copy, V, 0, 0)
            copy_small(dve, copy, V, 0, range(1, SU), first=True)
            copy_units(dve, copy, V, 0, 0)
            gram_rows(0, 0)
            next_one_hot(0)
            with dve.Fori(0, PAIRS - 1) as i:
                copy_groups(dve, copy, V, i, 1)
                copy_units(dve, copy, V, i, 1)
                copy_pairs(i, 0)
                copy_small(dve, copy, V, i + 1, [0])
                copy_groups(dve, copy, V, i + 1, 0)
                gram_rows(i, 1)
                copy_small(dve, copy, V, i + 1, range(1, SU))
                copy_pairs(i, 1)
                copy_units(dve, copy, V, i + 1, 0)
                gram_rows(i + 1, 0)
                next_one_hot(i + 1)
                copy_y(i)
            copy_groups(dve, copy, V, PAIRS - 1, 1)
            copy_units(dve, copy, V, PAIRS - 1, 1)
            copy_pairs(PAIRS - 1, 0)
            gram_rows(PAIRS - 1, 1)
            copy_pairs(PAIRS - 1, 1)
            copy_y(PAIRS - 1)


SMALL = [0, 4, 7, 9, 16]


def kernel(**inputs):
    import numpy as np
    import concourse.bacc as bacc
    from concourse.bass_utils import run_bass_kernel_spmd

    F, H, PAIR = 27, 13, 256
    gathered = [t for t in range(F - 1) if t not in SMALL]
    feature = [0] + [1 + t for t in gathered] + [1 + t for t in SMALL]
    place = {pair: n for n, pair in enumerate(zip(*np.triu_indices(F, k=1)))}
    order = [place[tuple(sorted((feature[f], feature[(f + o) % F])))] for f in range(F) for o in range(1, H + 1)]
    w1 = np.asarray(inputs["W_top1"])
    ids = np.asarray(inputs["ids"])
    ids_small = np.pad(ids[:, SMALL].T, ((0, 0), (0, PAIR)))
    arrays = {"bottom": inputs["r_bottom_output"], "ids": ids[:, gathered], "ids_small": ids_small}
    for t in range(F - 1):
        arrays[f"table{t}"] = inputs[f"tbl_{t}"]
    arrays |= {"w1": np.concatenate([w1[order], w1[len(order):]]), "b1": inputs["b_top1"],
               "w2": inputs["W_top2"], "b2": inputs["b_top2"], "w3": inputs["W_top3"]}
    arrays = {name: np.ascontiguousarray(a) for name, a in arrays.items()}

    nc = bacc.Bacc("TRN2", target_bir_lowering=False, num_devices=1)
    ap = {name: nc.dram_tensor(name, a.shape, mybir.dt.from_np(a.dtype), kind="ExternalInput").ap()
          for name, a in arrays.items()}
    out = nc.dram_tensor("out", (arrays["bottom"].shape[0], 1), mybir.dt.float32, kind="ExternalOutput").ap()
    dlrm_tower(nc, ap["bottom"], ap["ids"], ap["ids_small"], [ap[f"table{t}"] for t in gathered],
               [ap[f"table{t}"] for t in SMALL], ap["w1"], ap["b1"], ap["w2"], ap["b2"], ap["w3"], out)
    r = run_bass_kernel_spmd(nc, [arrays], core_ids=[0])
    return r.results[0]["out"]
```

```python
import concourse.bass as bass
from concourse import mybir
from contextlib import ExitStack

def dlrm_tower(nc, bottom, ids, ids_small, tables, small, w1, b1, w2, b2, w3, out):
    fp32 = mybir.dt.float32
    i32 = mybir.dt.int32
    i16 = mybir.dt.int16
    u16 = mybir.dt.uint16
    bf16 = mybir.dt.bfloat16
    ALU = mybir.AluOpType
    ACT = mybir.ActivationFunctionType

    B, D = bottom.shape
    NT = len(tables)
    NS = len(small)
    F = 1 + NT + NS
    P = 128
    TILES = B // P
    PAIRS = TILES // 2
    GF = 4
    GROUPS = (1 + NT + GF - 1) // GF
    FP = 32
    H = F // 2
    W = F + H
    Q = 32
    KT = 3
    KP = F * H // KT
    N1, N2 = w1.shape[1], w2.shape[1]
    C1, C2 = N1 // P, N2 // P
    NP = 2 * P
    PARTS = 3
    SC = 8
    SP = small[0].shape[0] // SC
    SU = (NS + 1) // 2
    SG = P // FP
    UG = 8
    UNITS = Q // UG
    RB = 4

    A, V = "scalar", "vector"
    GROUP_BY = [V, A, A, V, A, A, V][:GROUPS]
    SMALL_BY = [A, V, A, V][:SU]
    UNIT_BY = [A, V] * (UNITS // 2)
    def T(k, *groups):
        return [(("group", k, g), 1) for g in groups]

    STEP = [(("z", 0), 0), (("small", 0), 1), *T(0, 0, 1), (("small", 1), 1), *T(0, 2, 3), (("z", 1), 0),
            (("small", 2), 1), *T(0, 4, 5), (("h1", 0), 0), (("h1", 1), 0), *T(1, 0, 1), (("h2", 0), 0),
            *T(1, 2, 3), (("h2", 1), 0), *T(1, 4, 5), (("y", 0), 0)]
    FIRST = [(n, 0) for n in (("group", 0, 0), ("group", 0, 1), ("small", 0), ("group", 0, 2), ("group", 0, 3),
                              ("small", 1), ("group", 0, 4), ("group", 0, 5), ("small", 2),
                              *[("group", 1, g) for g in range(GROUPS)])]
    MLP = (("h1", 0), ("h1", 1), ("h2", 0), ("h2", 1), ("y", 0))
    LAST = [(("z", 0), 0)] + [(name, 0) for name in MLP] + [(("z", 1), 0)] + [(name, 1) for name in MLP]
    NAMES = [name for name, _ in STEP]
    BANK = {name: n % RB for n, name in enumerate(NAMES)}
    BANK["y", 0] = BANK["h2", 1]
    BY = {("z", 0): V, ("z", 1): V, ("h1", 0): A, ("h1", 1): A, ("h2", 0): A, ("h2", 1): A, ("y", 0): V}
    BY |= {("small", u): SMALL_BY[u] for u in range(SU)}
    BY |= {("group", k, g): GROUP_BY[g] for k in range(2) for g in range(GROUPS)}
    AHEAD = ("z", "h1", "h2", "y")
    assert len(GROUP_BY) == GROUPS and GROUPS == 6 and SU == 3 and F <= FP and C1 == 4 and C2 == 2 and 2 * NP == 512

    ctx = ExitStack()
    with ctx:
        def sb(name, shape, dt):
            return ctx.enter_context(nc.sbuf_tensor(name, shape, dt))

        def sem(name):
            return ctx.enter_context(nc.semaphore(name))

        ident = sb("ident", [P, P], fp32)
        ident_b = sb("ident_b", [P, P], bf16)
        idx = sb("idx", [P, 2, NT], i32)
        e = sb("e", [P, 2, 1 + NT, D], fp32)
        eT = sb("eT", [P, 2, P, FP], fp32)
        rT = sb("rT", [P, NP], fp32)
        parts = sb("parts", [SP, NS, PARTS, SC, D], bf16)
        row_of = sb("row_of", [SP, SC], fp32)
        row_of_i = sb("row_of_i", [SP, SC], i32)
        ids_b = sb("ids_b", [P, NS, NP], i32)
        ids_h = sb("ids_h", [P, NS, NP], i16)
        onehot = sb("onehot", [SP, SC, NS, NP], bf16)
        gr = sb("gr", [P, 2, Q, F], fp32)
        z = sb("z", [P, 2, Q, W], fp32)
        zc = sb("zc", [P, 2, F * H], fp32)
        zT = sb("zT", [KP, KT, NP], fp32)
        w1z = sb("w1z", [KP, KT, N1], fp32)
        w1r = sb("w1r", [D, N1], fp32)
        w2s = sb("w2s", [P, C1, N2], fp32)
        w3s = sb("w3s", [P, C2], fp32)
        b1s = sb("b1s", [P, C1], fp32)
        b2s = sb("b2s", [P, C2], fp32)
        h1 = sb("h1", [P, C1, NP], fp32)
        h2 = sb("h2", [P, C2, NP], fp32)
        whole = sb("whole", [SP, NS, SC, D], fp32)
        y = whole[:].rearrange("p j c d -> p (j c d)")[0:1, 0:B]

        ring = [ctx.enter_context(nc.psum_tensor(f"ring{i}", [P, 512], fp32)) for i in range(RB)]
        gram = [ctx.enter_context(nc.psum_tensor(f"gram{i}", [P, 2, 512], fp32)) for i in range(2)]

        s_ident0 = sem("ident_cleared")
        s_ident = sem("ident_ready")
        s_ident_b = sem("ident_b_ready")
        s_w = sem("weights_loaded")
        s_idx = [sem(f"idx_loaded{k}") for k in range(2)]
        s_r = [sem(f"bottom_loaded{k}") for k in range(2)]
        s_g = [[sem(f"gathered{k}_{g}") for g in range(GROUPS)] for k in range(2)]
        s_tr = sem("group_transposed")
        s_copied = {key: sem(f"{key[0]}_copied_by_{key[1]}") for key in sorted({(n[0], BY[n]) for n in NAMES})}
        s_gram = sem("gram_done")
        s_z = sem("z_ready")
        s_iota = sem("rows_numbered")
        s_row_of = sem("row_of_ready")
        s_ids_b = sem("small_ids_loaded")
        s_ids_h = sem("small_ids_narrowed")
        s_onehot = sem("onehot_ready")
        s_tab = [sem(f"small_table_loaded{j}") for j in range(NS)]
        s_split = [sem(f"split_steps{j}") for j in range(NS)]
        s_pad = sem("eT_padding_cleared")
        s_small = sem("small_summed")
        s_unit = {A: sem("unit_copied_by_scalar"), V: sem("unit_copied_by_vector")}
        s_zc = sem("pairs_packed")
        s_zp = sem("z_transposed")
        s_h1p = sem("h1_summed")
        s_h2p = sem("h2_summed")
        s_yp = sem("y_summed")
        s_out = sem("out_stored")
        s_tile_turn = sem("tile_turn")
        s_group_turn = sem("group_turn")

        def slots(g):
            return range(GF * g, min(GF * (g + 1), 1 + NT))

        def bank(name):
            return ring[BANK[name]]

        def key(name):
            return name[0], BY[name]

        def copied(i, name):
            same = sorted(n for n in NAMES if key(n) == key(name))
            return i * len(same) + (same.index(name) + 1 + len(same) * (name[0] in AHEAD))

        def wait_copied(engine, i, *names):
            for k in sorted({key(n) for n in names}):
                engine.wait_ge(s_copied[k], copied(i, max(n for n in names if key(n) == k)))

        def z_pairs(k):
            flat = z[:, k, :, :].rearrange("p f w -> p (f w)")
            skew = flat[:, 0:(Q * W) // (W + 1) * (W + 1)].rearrange("p (f w) -> p f w", w=W + 1)
            return skew[:, 0:F, 1:H + 1]

        def group_copy(copy, k, g):
            n = 2 * len(slots(g))
            src = bank(("group", k, g))[:, :].bitcast(u16)[:, 0:n * P].rearrange("p (f b) -> p b f", f=n)
            return copy(eT16[:, k, :, 2 * GF * g:2 * GF * g + n], src)

        def small_copy(copy, u):
            n = min(2, NS - 2 * u)
            f = 1 + NT + 2 * u
            src = bank(("small", u))[:, 0:n * NP].rearrange("p (f b) -> p b f", f=n)
            return copy(eT[:].rearrange("p k b f -> p (k b) f")[:, :, f:f + n], src)

        eT16 = eT[:].rearrange("p k b f -> p (k b f)").bitcast(u16).rearrange("p (k b f) -> p k b f", k=2, b=P)
        e16 = e[:].rearrange("p k s d -> p (k s d)").bitcast(bf16).rearrange("p (k s d h) -> p k s h d", k=2, d=D, h=2)

        ids_t = ids.rearrange("(t p) f -> t p f", p=P)
        bottom_t = bottom.rearrange("(t p) d -> t p d", p=P)

        block = ctx.enter_context(nc.Block())

        @block.sync
        def _(sp):
            def load_tile(t, k):
                sp.dma_start(idx[:, k, :], ids_t[t]).then_inc(s_idx[k], 16)
                sp.dma_start(e[:, k, 0, :], bottom_t[t]).then_inc(s_r[k], 16)

            def load_small_ids(i):
                src = ids_small[:, bass.ds(i * NP, NP)].rearrange("(o j) b -> o j b", o=1)
                sp.dma_start(ids_b[:], src.to_broadcast([P, NS, NP])).then_inc(s_ids_b, 16)

            load_tile(0, 0)
            load_small_ids(0)
            for j in range(NS):
                sp.dma_start(whole[:, j], small[j].rearrange("(p c) d -> p c d", c=SC)).then_inc(s_tab[j], 16)
            load_tile(1, 1)
            sp.wait_ge(s_ids_h, 1)
            load_small_ids(1)
            sp.wait_ge(s_tr, GROUPS)
            sp.dma_start(w1z[:], w1[0:KT * KP, :].rearrange("(m p) n -> p m n", p=KP)).then_inc(s_w, 16)
            sp.dma_start(w1r[:], w1[KT * KP:KT * KP + D, :]).then_inc(s_w, 16)
            sp.dma_start(w2s[:], w2.rearrange("(c p) n -> p c n", p=P)).then_inc(s_w, 16)
            with nc.allow_non_contiguous_dma(reason="small vectors"):
                sp.dma_start(w3s[:], w3.rearrange("(c p) o -> p (c o)", p=P)).then_inc(s_w, 16)
                sp.dma_start(b1s[:], b1.rearrange("(c p) -> p c", p=P)).then_inc(s_w, 16)
                sp.dma_start(b2s[:], b2.rearrange("(c p) -> p c", p=P)).then_inc(s_w, 16)
            with sp.Fori(1, PAIRS) as i:
                for k in range(2):
                    sp.wait_ge(s_tr, (i - 1) * (2 * GROUPS) + (k + 1) * GROUPS)
                    sp.sem_inc(s_tile_turn, 1)
                    load_tile(i * 2 + k, k)
                    if k == 0:
                        sp.wait_ge(s_ids_h, i + 1)
                        sp.sem_inc(s_tile_turn, 1)
                        load_small_ids(i + 1)
            wait_copied(sp, PAIRS, ("y", 0))
            sp.dma_start(out.rearrange("b o -> o b"), y).then_inc(s_out, 16)
            sp.wait_ge(s_out, 16)

        @block.gpsimd
        def _(pool):
            nc.gpsimd.memset(ident[:], 0.0).then_inc(s_ident0, 1)
            pool.wait_ge(s_ident0, 1)
            nc.gpsimd.affine_select(out=ident[:], in_=ident[:], compare_op=ALU.not_equal, fill=1.0,
                                    base=0, pattern=[[-1, P]], channel_multiplier=1).then_inc(s_ident, 1)
            nc.gpsimd.iota(row_of_i[:], pattern=[[1, SC]], base=0, channel_multiplier=SC).then_inc(s_iota, 1)

            def gathers(i, k, first):
                pool.wait_ge(s_idx[k], i * 16 + 16)
                pool.sem_inc(s_group_turn, 1)
                for g in range(GROUPS):
                    if not first:
                        pool.wait_ge(s_tr, (i - 1) * (2 * GROUPS) + (k * GROUPS + g + 1))
                        pool.sem_inc(s_group_turn, 1)
                    for s in slots(g):
                        if s:
                            nc.gpsimd.indirect_dma_start(
                                out=e[:, k, s, :], out_offset=None, in_=tables[s - 1],
                                in_offset=bass.IndirectOffsetOnAxis(ap=idx[:, k, s - 1:s], axis=0),
                            ).then_inc(s_g[k][g], 16)

            for k in range(2):
                gathers(0, k, True)
            with pool.Fori(1, PAIRS) as i:
                for k in range(2):
                    gathers(i, k, False)

        @block.tensor
        def _(pe):
            def take(i, name, part=STEP):
                step = i - dict(STEP)[name] if part is STEP else 0 if part is FIRST else PAIRS - 1
                n = [m for m, _ in part].index(name) if part is STEP else part.index((name, i - step))
                before = [(m, step + ahead) for m, ahead in part[:n] if BANK[m] == BANK[name]]
                if part is not FIRST:
                    before = [(m, step - 1 + ahead) for m, ahead in STEP if BANK[m] == BANK[name]] + before
                if before:
                    m, pair = before[-1]
                    pe.wait_ge(s_copied[key(m)], copied(pair, m))
                return bank(name)

            def small_tables(i, uses, part=STEP):
                pe.wait_ge(s_onehot, i * 2 + 2)
                for u in uses:
                    dst = take(i, ("small", u), part)
                    for n in range(min(2, NS - 2 * u)):
                        j = 2 * u + n
                        if part is FIRST:
                            pe.wait_ge(s_split[j], 4)
                        for m in range(PARTS):
                            for c in range(SC):
                                last = nc.tensor.matmul(dst[:, n * NP:(n + 1) * NP], parts[:, j, m, c, :],
                                                        onehot[:, c, j, :], start=m == 0 and c == 0,
                                                        stop=m == PARTS - 1 and c == SC - 1)
                    last.then_inc(s_small, 1)

            def transposes(i, k, groups=range(GROUPS), part=STEP):
                if 0 in groups:
                    pe.wait_ge(s_r[k], i * 16 + 16)
                for g in groups:
                    pe.wait_ge(s_g[k][g], (i + 1) * (16 * len([s for s in slots(g) if s])))
                    dst = take(i, ("group", k, g), part)
                    for n, s in enumerate(slots(g)):
                        for h in range(2):
                            at = (2 * n + h) * P
                            last = nc.tensor.transpose(dst[:, :].bitcast(bf16)[:, at:at + P], e16[:, k, s, h, :],
                                                       ident_b[:])
                    last.then_inc(s_tr, 1)

            def grams(i, k):
                wait_copied(pe, i, *[("small", u) for u in range(SU)], *[("group", k, g) for g in range(GROUPS)])
                for u in range(UNITS):
                    pe.wait_ge(s_unit[UNIT_BY[u]], i * UNITS + (k * UNITS // 2 + u // 2 + 1))
                    for n in range(UG):
                        v = eT[:, k, SG * (UG * u + n):SG * (UG * u + n + 1), :]
                        per = UG // 2
                        col = n % per * SG * F
                        last = nc.tensor.matmul(gram[u % 2][:, n // per, col:col + SG * F],
                                                v.rearrange("p s f -> p (s f)"), v[:, :, 0:F],
                                                start=True, stop=True, skip_group_check=True)
                    last.then_inc(s_gram, 1)

            def z_transposes(i, k, part=STEP):
                pe.wait_ge(s_zc, i * 2 + (k + 1))
                dst = take(i, ("z", k), part)
                for m in range(KT):
                    last = nc.tensor.transpose(dst[0:KP, m * P:(m + 1) * P], zc[:, k, m * KP:(m + 1) * KP], ident[:])
                last.then_inc(s_zp, 1)


            def layer1(i, u, samples=slice(0, NP), part=STEP):
                dst = take(i, ("h1", u), part)
                for v in range(2):
                    c = 2 * u + v
                    o = dst[:, v * NP:(v + 1) * NP][:, samples]
                    for m in range(KT):
                        nc.tensor.matmul(o, w1z[:, m, c * P:(c + 1) * P], zT[:, m, samples], start=m == 0, stop=False)
                    last = nc.tensor.matmul(o, w1r[:, c * P:(c + 1) * P], rT[:, samples], start=False, stop=True)
                last.then_inc(s_h1p, 1)

            def layer2(i, v, samples=slice(0, NP), part=STEP):
                dst = take(i, ("h2", v), part)
                for c in range(C1):
                    if v == 0 and c % 2 == 0:
                        wait_copied(pe, i, ("h1", c // 2))
                    last = nc.tensor.matmul(dst[:, samples], w2s[:, c, v * P:(v + 1) * P], h1[:, c, samples],
                                            start=c == 0, stop=c == C1 - 1)
                last.then_inc(s_h2p, 1)

            def layer3(i, samples=slice(0, NP), part=STEP):
                dst = take(i, ("y", 0), part)
                for c in range(C2):
                    wait_copied(pe, i, ("h2", c))
                    last = nc.tensor.matmul(dst[0:1, samples], w3s[:, c:c + 1], h2[:, c, samples],
                                            start=c == 0, stop=c == C2 - 1)
                last.then_inc(s_yp, 1)

            pe.wait_ge(s_ident, 1)
            pe.wait_ge(s_ident_b, 1)
            pe.wait_ge(s_pad, 1)
            transposes(0, 0, [0, 1], FIRST)
            small_tables(0, [0], FIRST)
            transposes(0, 0, [2, 3], FIRST)
            small_tables(0, [1], FIRST)
            transposes(0, 0, [4, 5], FIRST)
            small_tables(0, [2], FIRST)
            grams(0, 0)
            transposes(0, 1, part=FIRST)
            with pe.Fori(0, PAIRS - 1) as i:
                z_transposes(i, 0)
                small_tables(i + 1, [0])
                grams(i, 1)
                transposes(i + 1, 0, [0, 1])
                small_tables(i + 1, [1])
                transposes(i + 1, 0, [2, 3])
                z_transposes(i, 1)
                small_tables(i + 1, [2])
                transposes(i + 1, 0, [4, 5])
                wait_copied(pe, i, ("z", 0), ("z", 1))
                pe.wait_ge(s_w, 16 * 6)
                layer1(i, 0)
                grams(i + 1, 0)
                layer1(i, 1)
                transposes(i + 1, 1, [0, 1])
                layer2(i, 0)
                transposes(i + 1, 1, [2, 3])
                layer2(i, 1)
                transposes(i + 1, 1, [4, 5])
                layer3(i)
            z_transposes(PAIRS - 1, 0, LAST)
            grams(PAIRS - 1, 1)
            for k in range(2):
                if k:
                    z_transposes(PAIRS - 1, k, LAST)
                wait_copied(pe, PAIRS - 1, ("z", k))
                at = PAIRS - 1 + k, slice(k * P, (k + 1) * P), LAST
                layer1(at[0], 0, *at[1:])
                layer1(at[0], 1, *at[1:])
                layer2(at[0], 0, *at[1:])
                layer2(at[0], 1, *at[1:])
                layer3(*at)


        def copy_small(engine, copy, by, i, uses, first=False):
            for u in uses:
                if SMALL_BY[u] == by:
                    if not first:
                        engine.wait_ge(s_gram, i * (2 * UNITS))
                    engine.wait_ge(s_small, i * SU + (u + 1))
                    small_copy(copy, u).then_inc(s_copied["small", by], 1)

        def copy_groups(engine, copy, by, i, k, groups=range(GROUPS)):
            for g in groups:
                if GROUP_BY[g] == by:
                    if g == 0:
                        wait_copied(engine, i - 1, ("z", k))
                    engine.wait_ge(s_tr, i * (2 * GROUPS) + (k * GROUPS + g + 1))
                    group_copy(copy, k, g).then_inc(s_copied["group", by], 1)

        def copy_units(engine, copy, by, i, k):
            engine.wait_ge(s_z, i * 2 + (k + 1))
            for u in range(UNITS):
                if UNIT_BY[u] == by:
                    engine.wait_ge(s_gram, i * (2 * UNITS) + (k * UNITS + u + 1))
                    for s in range(SG):
                        rows = slice(FP * s, FP * (s + 1))
                        src = gram[u % 2][rows, :, 0:UG // 2 * SG * F].rearrange("p h (g w) -> p h g w", w=SG * F)
                        dst = gr[rows, k, UG * u:UG * (u + 1), :].rearrange("p (h g) f -> p h g f", h=2)
                        last = copy(dst, src[:, :, :, s * F:(s + 1) * F])
                    last.then_inc(s_unit[by], 1)

        @block.scalar
        def _(act):
            act.sem_inc(s_copied["h1", A], 2)
            act.sem_inc(s_copied["h2", A], 2)
            act.sem_inc(s_unit[A], 1)

            def pack(i, k):
                act.wait_ge(s_z, i * 2 + (k + 3))
                nc.scalar.copy(zc[:, k, :].rearrange("p (f o) -> p f o", f=F), z_pairs(k)).then_inc(s_zc, 1)

            def relu1(i, u, samples=slice(0, NP)):
                act.wait_ge(s_w, 16 * 6)
                act.wait_ge(s_h1p, i * 2 + (u + 1))
                for v in range(2):
                    c = 2 * u + v
                    last = nc.scalar.activation(h1[:, c, samples], bank(("h1", u))[:, v * NP:(v + 1) * NP][:, samples],
                                                ACT.Relu, bias=b1s[:, c:c + 1])
                last.then_inc(s_copied["h1", A], 1)

            def relu2(i, v, samples=slice(0, NP)):
                act.wait_ge(s_h2p, i * C2 + (v + 1))
                nc.scalar.activation(h2[:, v, samples], bank(("h2", v))[:, samples], ACT.Relu,
                                     bias=b2s[:, v:v + 1]).then_inc(s_copied["h2", A], 1)

            def head(j):
                act.wait_ge(s_tab[j], 16)
                nc.scalar.copy(parts[:, j, 0], whole[:, j]).then_inc(s_split[j], 1)

            def middle(j):
                act.wait_ge(s_split[j], 2)
                nc.scalar.copy(parts[:, j, 1], whole[:, j]).then_inc(s_split[j], 1)

            copy = nc.scalar.copy
            for j in (0, 1, 2, 3):
                head(j)
            middle(0)
            middle(1)
            head(4)
            copy_groups(act, copy, A, 0, 0, [1])
            middle(2)
            middle(3)
            copy_small(act, copy, A, 0, [0], first=True)
            copy_groups(act, copy, A, 0, 0, [2])
            middle(4)
            copy_groups(act, copy, A, 0, 0, [4, 5])
            copy_small(act, copy, A, 0, [2], first=True)
            copy_units(act, copy, A, 0, 0)
            copy_groups(act, copy, A, 0, 1)
            pack(0, 0)
            with act.Fori(0, PAIRS - 1) as i:
                copy_units(act, copy, A, i, 1)
                copy_small(act, copy, A, i + 1, [0])
                copy_groups(act, copy, A, i + 1, 0, [1])
                pack(i, 1)
                copy_groups(act, copy, A, i + 1, 0, [2])
                copy_small(act, copy, A, i + 1, [2])
                copy_groups(act, copy, A, i + 1, 0, [4, 5])
                relu1(i, 0)
                copy_units(act, copy, A, i + 1, 0)
                relu1(i, 1)
                pack(i + 1, 0)
                copy_groups(act, copy, A, i + 1, 1, [1])
                relu2(i, 0)
                copy_groups(act, copy, A, i + 1, 1, [2])
                relu2(i, 1)
                copy_groups(act, copy, A, i + 1, 1, [4, 5])
            copy_units(act, copy, A, PAIRS - 1, 1)
            for k in range(2):
                if k == 1:
                    pack(PAIRS - 1, 1)
                samples = slice(k * P, (k + 1) * P)
                relu1(PAIRS - 1 + k, 0, samples)
                relu1(PAIRS - 1 + k, 1, samples)
                relu2(PAIRS - 1 + k, 0, samples)
                relu2(PAIRS - 1 + k, 1, samples)

        @block.vector
        def _(dve):
            copy = nc.vector.tensor_copy
            dve.sem_inc(s_z, 2)
            dve.sem_inc(s_copied["z", V], 2)
            dve.sem_inc(s_copied["y", V], 1)
            dve.sem_inc(s_unit[V], 1)

            def narrow_ids(i):
                dve.wait_ge(s_ids_b, i * 16 + 16)
                copy(ids_h[:], ids_b[:]).then_inc(s_ids_h, 1)
                dve.wait_ge(s_ids_h, i + 1)

            def one_hot(chunks):
                for c in chunks:
                    last = nc.vector.tensor_scalar(onehot[:, c], ids_h[0:SP], row_of[:, c:c + 1], None, ALU.is_equal)
                last.then_inc(s_onehot, 1)

            dve.wait_ge(s_ident, 1)
            copy(ident_b[:], ident[:]).then_inc(s_ident_b, 1)
            nc.vector.memset(eT[:, :, :, F:FP], 0.0).then_inc(s_pad, 1)
            dve.wait_ge(s_iota, 1)
            copy(row_of[:], row_of_i[:]).then_inc(s_row_of, 1)
            dve.wait_ge(s_row_of, 1)
            narrow_ids(0)
            one_hot(range(SC // 2))
            one_hot(range(SC // 2, SC))

            def less(j, part):
                dve.wait_ge(s_split[j], 2 * part + 1)
                dst = parts[:, j, 2] if part else whole[:, j]
                nc.vector.tensor_tensor(dst, whole[:, j], parts[:, j, part], ALU.subtract).then_inc(s_split[j], 1)

            def gram_rows(i, k):
                for by in (A, V):
                    dve.wait_ge(s_unit[by], i * UNITS + ((k + 1) * UNITS // 2 + 1))
                nc.vector.transpose(z[:, k, :, 0:F].rearrange("p f g -> p g f"),
                                    gr[:, k].rearrange("p q g -> p g q"))
                nc.vector.transpose(z[:, k, :, F:W].rearrange("p f g -> p g f"),
                                    gr[:, k, :, 0:H].rearrange("p q g -> p g q")).then_inc(s_z, 1)

            def copy_pairs(i, k):
                dve.wait_ge(s_zp, i * 2 + (k + 1))
                src = bank(("z", k))[0:KP, 0:KT * P].rearrange("p (m s q) -> p m q s", m=KT, s=SG)
                dst = zT[:, :, k * P:(k + 1) * P].rearrange("p m (q s) -> p m q s", s=SG)
                copy(rT[:, k * P:(k + 1) * P], eT[:, k, :, 0])
                copy(dst, src).then_inc(s_copied["z", V], 1)

            def copy_y(i, at, samples=slice(0, NP)):
                dve.wait_ge(s_yp, i + 1)
                dst = y[:, bass.ds(at, samples.stop - samples.start)]
                copy(dst, bank(("y", 0))[0:1, samples]).then_inc(s_copied["y", V], 1)

            def next_ids(i):
                dve.wait_ge(s_small, i * SU + SU)
                narrow_ids(i + 1)

            less(0, 0)
            less(1, 0)
            less(0, 1)
            less(1, 1)
            copy_groups(dve, copy, V, 0, 0, [0])
            less(2, 0)
            less(3, 0)
            less(2, 1)
            less(3, 1)
            less(4, 0)
            copy_groups(dve, copy, V, 0, 0, [3])
            less(4, 1)
            copy_small(dve, copy, V, 0, [1], first=True)
            next_ids(0)
            one_hot(range(SC // 2))
            one_hot(range(SC // 2, SC))
            copy_units(dve, copy, V, 0, 0)
            gram_rows(0, 0)
            copy_groups(dve, copy, V, 0, 1)
            with dve.Fori(0, PAIRS - 1) as i:
                copy_pairs(i, 0)
                copy_units(dve, copy, V, i, 1)
                gram_rows(i, 1)
                copy_groups(dve, copy, V, i + 1, 0, [0])
                copy_small(dve, copy, V, i + 1, [1])
                copy_groups(dve, copy, V, i + 1, 0, [3])
                copy_pairs(i, 1)
                copy_units(dve, copy, V, i + 1, 0)
                gram_rows(i + 1, 0)
                next_ids(i + 1)
                one_hot(range(SC // 2))
                copy_groups(dve, copy, V, i + 1, 1, [0])
                one_hot(range(SC // 2, SC))
                copy_groups(dve, copy, V, i + 1, 1, [3])
                copy_y(i, i * NP)
            copy_pairs(PAIRS - 1, 0)
            copy_units(dve, copy, V, PAIRS - 1, 1)
            gram_rows(PAIRS - 1, 1)
            for k in range(2):
                if k == 1:
                    copy_pairs(PAIRS - 1, 1)
                copy_y(PAIRS - 1 + k, (2 * PAIRS - 2 + k) * P, slice(k * P, (k + 1) * P))


SMALL = [0, 4, 7, 9, 16]


def kernel(**inputs):
    import numpy as np
    import concourse.bacc as bacc
    from concourse.bass_utils import run_bass_kernel_spmd

    F, H, PAIR = 27, 13, 256
    gathered = [t for t in range(F - 1) if t not in SMALL]
    feature = [0] + [1 + t for t in gathered] + [1 + t for t in SMALL]
    place = {pair: n for n, pair in enumerate(zip(*np.triu_indices(F, k=1)))}
    order = [place[tuple(sorted((feature[f], feature[(f + o) % F])))] for f in range(F) for o in range(1, H + 1)]
    w1 = np.asarray(inputs["W_top1"])
    ids = np.asarray(inputs["ids"])
    ids_small = np.pad(ids[:, SMALL].T, ((0, 0), (0, PAIR)))
    arrays = {"bottom": inputs["r_bottom_output"], "ids": ids[:, gathered], "ids_small": ids_small}
    for t in range(F - 1):
        arrays[f"table{t}"] = inputs[f"tbl_{t}"]
    arrays |= {"w1": np.concatenate([w1[order], w1[len(order):]]), "b1": inputs["b_top1"],
               "w2": inputs["W_top2"], "b2": inputs["b_top2"], "w3": inputs["W_top3"]}
    arrays = {name: np.ascontiguousarray(a) for name, a in arrays.items()}

    nc = bacc.Bacc("TRN2", target_bir_lowering=False, num_devices=1)
    ap = {name: nc.dram_tensor(name, a.shape, mybir.dt.from_np(a.dtype), kind="ExternalInput").ap()
          for name, a in arrays.items()}
    out = nc.dram_tensor("out", (arrays["bottom"].shape[0], 1), mybir.dt.float32, kind="ExternalOutput").ap()
    dlrm_tower(nc, ap["bottom"], ap["ids"], ap["ids_small"], [ap[f"table{t}"] for t in gathered],
               [ap[f"table{t}"] for t in SMALL], ap["w1"], ap["b1"], ap["w2"], ap["b2"], ap["w3"], out)
    r = run_bass_kernel_spmd(nc, [arrays], core_ids=[0])
    return r.results[0]["out"]
```

```python
import concourse.bass as bass
from concourse import mybir
from contextlib import ExitStack

def dlrm_tower(nc, bottom, ids, ids_small, tables, small, w1, b1, w2, b2, w3, out):
    fp32 = mybir.dt.float32
    i32 = mybir.dt.int32
    i16 = mybir.dt.int16
    u16 = mybir.dt.uint16
    bf16 = mybir.dt.bfloat16
    ALU = mybir.AluOpType
    ACT = mybir.ActivationFunctionType

    B, D = bottom.shape
    NT = len(tables)
    NS = len(small)
    F = 1 + NT + NS
    P = 128
    TILES = B // P
    PAIRS = TILES // 2
    GF = 4
    GROUPS = (1 + NT + GF - 1) // GF
    FP = 32
    H = F // 2
    W = F + H
    Q = 32
    KT = 3
    KP = F * H // KT
    N1, N2 = w1.shape[1], w2.shape[1]
    C1, C2 = N1 // P, N2 // P
    NP = 2 * P
    PARTS = 3
    SC = 8
    SP = small[0].shape[0] // SC
    SU = (NS + 1) // 2
    SG = P // FP
    UG = 8
    UNITS = Q // UG
    RB = 4

    A, V = "scalar", "vector"
    BANK = {("group", 0, 0): 0, ("group", 0, 1): 2, ("small", 1): 3, ("group", 0, 2): 1, ("group", 0, 3): 0,
            ("small", 2): 2, ("h1", 0): 3, ("h1", 1): 1, ("group", 0, 4): 0, ("group", 0, 5): 2, ("h2", 0): 3,
            ("group", 1, 0): 1, ("group", 1, 1): 0, ("group", 1, 2): 3, ("h2", 1): 2, ("group", 1, 3): 0,
            ("small", 0): 1, ("group", 1, 4): 3, ("group", 1, 5): 2, ("y", 0): 0}
    NAMES = [*BANK, ("z", 0), ("z", 1)]
    GROUP_BY = [V, A, A, V, A, V]
    SMALL_BY = [A, V, A]
    UNIT_BY = [A, V] * (UNITS // 2)
    BY = {("z", 0): V, ("z", 1): V, ("h1", 0): A, ("h1", 1): A, ("h2", 0): A, ("h2", 1): A, ("y", 0): V}
    BY |= {("small", u): SMALL_BY[u] for u in range(SU)}
    BY |= {("group", k, g): GROUP_BY[g] for k in range(2) for g in range(GROUPS)}
    AHEAD = ("z", "h1", "h2", "y")

    def groups(k, *numbers, ahead=1):
        return [(("group", k, g), ahead) for g in numbers]

    FIRST = [*groups(0, 0, ahead=0), (("small", 0), 0), *groups(0, 1, 2, 3, ahead=0), (("small", 1), 0),
             (("small", 2), 0), *groups(0, 4, 5, ahead=0), *groups(1, 0, 1, 2, 3, ahead=0), (("small", 0), 1),
             *groups(1, 4, 5, ahead=0)]
    STEP = [*groups(0, 0, 1), (("small", 1), 1), *groups(0, 2, 3), (("small", 2), 1), (("h1", 0), 0), (("h1", 1), 0),
            *groups(0, 4, 5), (("h2", 0), 0), *groups(1, 0, 1, 2), (("h2", 1), 0), *groups(1, 3),
            (("small", 0), 2), *groups(1, 4, 5), (("y", 0), 0)]
    LAST = STEP[:STEP.index((("small", 0), 2))]
    LAST += [*groups(1, 4, 5), (("y", 0), 0), (("h1", 0), 1), (("h1", 1), 1), (("h2", 0), 1),
             (("h2", 1), 1), (("h1", 0), 2), (("h1", 1), 2), (("y", 0), 1), (("h2", 0), 2), (("h2", 1), 2),
             (("y", 0), 2)]
    assert GROUPS == 6 and SU == 3 and F <= FP and C1 == 4 and C2 == 2 and 2 * NP == 512

    ctx = ExitStack()
    with ctx:
        def sb(name, shape, dt):
            return ctx.enter_context(nc.sbuf_tensor(name, shape, dt))

        def sem(name):
            return ctx.enter_context(nc.semaphore(name))

        ident = sb("ident", [P, P], fp32)
        ident_b = sb("ident_b", [P, P], bf16)
        idx = sb("idx", [P, 2, NT], i32)
        e = sb("e", [P, 2, 1 + NT, D], fp32)
        eT = sb("eT", [P, 2, P, FP], fp32)
        rT = sb("rT", [P, NP], fp32)
        whole = sb("whole", [SP, NS, SC, D], fp32)
        rest = sb("rest", [SP, NS, SC, D], fp32)
        last_part = sb("last_part", [SP, NS, SC, D], bf16)
        row_of = sb("row_of", [SP, SC], fp32)
        row_of_i = sb("row_of_i", [SP, SC], i32)
        ids_b = sb("ids_b", [P, NS, NP], i32)
        ids_h = sb("ids_h", [P, NS, NP], i16)
        onehot = sb("onehot", [SP, SC, NS, NP], bf16)
        gr = sb("gr", [P, 2, Q, F], fp32)
        z = sb("z", [P, 2, Q, W], fp32)
        zc = sb("zc", [P, 2, F * H], fp32)
        zT = sb("zT", [KP, KT, NP], fp32)
        w1z = sb("w1z", [KP, KT, N1], fp32)
        w1r = sb("w1r", [D, N1], fp32)
        w2s = sb("w2s", [P, C1, N2], fp32)
        w3s = sb("w3s", [P, C2], fp32)
        b1s = sb("b1s", [P, C1], fp32)
        b2s = sb("b2s", [P, C2], fp32)
        h1 = sb("h1", [P, C1, NP], fp32)
        h2 = sb("h2", [P, C2, NP], fp32)
        y = sb("y", [1, B], fp32)

        ring = [ctx.enter_context(nc.psum_tensor(f"ring{i}", [P, 512], fp32)) for i in range(RB)]
        gram = [ctx.enter_context(nc.psum_tensor(f"gram{i}", [P, 2, 512], fp32)) for i in range(2)]

        s_ident0 = sem("ident_cleared")
        s_ident = sem("ident_ready")
        s_ident_b = sem("ident_b_ready")
        s_w = sem("weights_loaded")
        s_idx = [sem(f"idx_loaded{k}") for k in range(2)]
        s_r = [sem(f"bottom_loaded{k}") for k in range(2)]
        s_g = [[sem(f"gathered{k}_{g}") for g in range(GROUPS)] for k in range(2)]
        s_tr = sem("group_transposed")
        s_copied = {key: sem(f"{key[0]}_copied_by_{key[1]}") for key in sorted({(n[0], BY[n]) for n in NAMES})}
        s_gram = sem("gram_done")
        s_z = sem("z_ready")
        s_iota = sem("rows_numbered")
        s_row_of = sem("row_of_ready")
        s_ids_b = sem("small_ids_loaded")
        s_ids_h = sem("small_ids_narrowed")
        s_onehot = sem("onehot_ready")
        s_tab = [sem(f"small_table_loaded{j}") for j in range(NS)]
        s_split = [sem(f"split_steps{j}") for j in range(NS)]
        s_pad = sem("eT_padding_cleared")
        s_small = sem("small_summed")
        s_unit = {A: sem("unit_copied_by_scalar"), V: sem("unit_copied_by_vector")}
        s_zc = sem("pairs_packed")
        s_zp = sem("z_transposed")
        s_h1p = sem("h1_summed")
        s_h2p = sem("h2_summed")
        s_yp = sem("y_summed")
        s_out = sem("out_stored")
        s_tile_turn = sem("tile_turn")
        s_group_turn = sem("group_turn")

        z_bank = gram[1][:, 0, :]

        def slots(g):
            return range(GF * g, min(GF * (g + 1), 1 + NT))

        def bank(name):
            return ring[BANK[name]]

        def key(name):
            return name[0], BY[name]

        def copied(i, name):
            same = sorted(n for n in NAMES if key(n) == key(name))
            return i * len(same) + (same.index(name) + 1 + len(same) * (name[0] in AHEAD))

        def wait_copied(engine, i, *names):
            for k in sorted({key(n) for n in names}):
                engine.wait_ge(s_copied[k], copied(i, max(n for n in names if key(n) == k)))

        def z_pairs(k):
            flat = z[:, k, :, :].rearrange("p f w -> p (f w)")
            skew = flat[:, 0:(Q * W) // (W + 1) * (W + 1)].rearrange("p (f w) -> p f w", w=W + 1)
            return skew[:, 0:F, 1:H + 1]

        def group_copy(copy, k, g):
            n = 2 * len(slots(g))
            src = bank(("group", k, g))[:, :].bitcast(u16)[:, 0:n * P].rearrange("p (f b) -> p b f", f=n)
            return copy(eT16[:, k, :, 2 * GF * g:2 * GF * g + n], src)

        def small_copy(copy, u):
            n = min(2, NS - 2 * u)
            f = 1 + NT + 2 * u
            src = bank(("small", u))[:, 0:n * NP].rearrange("p (f b) -> p b f", f=n)
            return copy(eT[:].rearrange("p k b f -> p (k b) f")[:, :, f:f + n], src)

        eT16 = eT[:].rearrange("p k b f -> p (k b f)").bitcast(u16).rearrange("p (k b f) -> p k b f", k=2, b=P)
        e16 = e[:].rearrange("p k s d -> p (k s d)").bitcast(bf16).rearrange("p (k s d h) -> p k s h d", k=2, d=D, h=2)

        def upper(words):
            halves = words[:].rearrange("p j c d -> p (j c d)").bitcast(bf16)
            return halves.rearrange("p (j c d h) -> p j c d h", j=NS, c=SC, h=2)[:, :, :, :, 1]

        parts = [upper(whole), upper(rest), last_part[:]]

        ids_t = ids.rearrange("(t p) f -> t p f", p=P)
        bottom_t = bottom.rearrange("(t p) d -> t p d", p=P)

        block = ctx.enter_context(nc.Block())

        @block.sync
        def _(sp):
            def load_tile(t, k):
                sp.dma_start(idx[:, k, :], ids_t[t]).then_inc(s_idx[k], 16)
                sp.dma_start(e[:, k, 0, :], bottom_t[t]).then_inc(s_r[k], 16)

            def load_small_ids(i):
                src = ids_small[:, bass.ds(i * NP, NP)].rearrange("(o j) b -> o j b", o=1)
                sp.dma_start(ids_b[:], src.to_broadcast([P, NS, NP])).then_inc(s_ids_b, 16)

            load_tile(0, 0)
            load_small_ids(0)
            for j in range(NS):
                sp.dma_start(whole[:, j], small[j].rearrange("(p c) d -> p c d", c=SC)).then_inc(s_tab[j], 16)
            load_tile(1, 1)
            sp.wait_ge(s_ids_h, 1)
            load_small_ids(1)
            sp.wait_ge(s_tr, GROUPS)
            sp.dma_start(w1z[:], w1[0:KT * KP, :].rearrange("(m p) n -> p m n", p=KP)).then_inc(s_w, 16)
            sp.dma_start(w1r[:], w1[KT * KP:KT * KP + D, :]).then_inc(s_w, 16)
            sp.dma_start(w2s[:], w2.rearrange("(c p) n -> p c n", p=P)).then_inc(s_w, 16)
            with nc.allow_non_contiguous_dma(reason="small vectors"):
                sp.dma_start(w3s[:], w3.rearrange("(c p) o -> p (c o)", p=P)).then_inc(s_w, 16)
                sp.dma_start(b1s[:], b1.rearrange("(c p) -> p c", p=P)).then_inc(s_w, 16)
                sp.dma_start(b2s[:], b2.rearrange("(c p) -> p c", p=P)).then_inc(s_w, 16)

            def next_loads(i, more):
                for k in range(2):
                    sp.wait_ge(s_tr, (i - 1) * (2 * GROUPS) + (k + 1) * GROUPS)
                    sp.sem_inc(s_tile_turn, 1)
                    load_tile(i * 2 + k, k)
                    if k == 0 and more:
                        sp.wait_ge(s_ids_h, i + 1)
                        sp.sem_inc(s_tile_turn, 1)
                        load_small_ids(i + 1)

            with sp.Fori(1, PAIRS - 1) as i:
                next_loads(i, True)
            next_loads(PAIRS - 1, False)
            wait_copied(sp, PAIRS, ("y", 0))
            sp.dma_start(out.rearrange("b o -> o b"), y[:]).then_inc(s_out, 16)
            sp.wait_ge(s_out, 16)

        @block.gpsimd
        def _(pool):
            nc.gpsimd.memset(ident[:], 0.0).then_inc(s_ident0, 1)
            pool.wait_ge(s_ident0, 1)
            nc.gpsimd.affine_select(out=ident[:], in_=ident[:], compare_op=ALU.not_equal, fill=1.0,
                                    base=0, pattern=[[-1, P]], channel_multiplier=1).then_inc(s_ident, 1)
            nc.gpsimd.iota(row_of_i[:], pattern=[[1, SC]], base=0, channel_multiplier=SC).then_inc(s_iota, 1)

            def gathers(i, k, first):
                pool.wait_ge(s_idx[k], i * 16 + 16)
                pool.sem_inc(s_group_turn, 1)
                for g in range(GROUPS):
                    if not first:
                        pool.wait_ge(s_tr, (i - 1) * (2 * GROUPS) + (k * GROUPS + g + 1))
                        pool.sem_inc(s_group_turn, 1)
                    for s in slots(g):
                        if s:
                            nc.gpsimd.indirect_dma_start(
                                out=e[:, k, s, :], out_offset=None, in_=tables[s - 1],
                                in_offset=bass.IndirectOffsetOnAxis(ap=idx[:, k, s - 1:s], axis=0),
                            ).then_inc(s_g[k][g], 16)

            for k in range(2):
                gathers(0, k, True)
            with pool.Fori(1, PAIRS) as i:
                for k in range(2):
                    gathers(i, k, False)

        @block.tensor
        def _(pe):
            def take(i, name, part=STEP):
                step = i - dict(STEP)[name] if part is STEP else 0 if part is FIRST else PAIRS - 2
                n = [m for m, _ in part].index(name) if part is STEP else part.index((name, i - step))
                before = [(m, step + ahead) for m, ahead in part[:n] if BANK[m] == BANK[name]]
                if part is not FIRST:
                    before = [(m, step - 1 + ahead) for m, ahead in STEP if BANK[m] == BANK[name]] + before
                if before:
                    m, pair = before[-1]
                    pe.wait_ge(s_copied[key(m)], copied(pair, m))
                return bank(name)

            def small_tables(i, uses, part=STEP):
                pe.wait_ge(s_onehot, i + 1)
                for u in uses:
                    dst = take(i, ("small", u), part)
                    for n in range(min(2, NS - 2 * u)):
                        j = 2 * u + n
                        if part is FIRST and i == 0:
                            pe.wait_ge(s_split[j], 2)
                        for m in range(PARTS):
                            for c in range(SC):
                                last = nc.tensor.matmul(dst[:, n * NP:(n + 1) * NP], parts[m][:, j, c, :],
                                                        onehot[:, c, j, :], start=m == 0 and c == 0,
                                                        stop=m == PARTS - 1 and c == SC - 1)
                    last.then_inc(s_small, 1)

            def transposes(i, k, groups=range(GROUPS), part=STEP):
                if 0 in groups:
                    pe.wait_ge(s_r[k], i * 16 + 16)
                for g in groups:
                    pe.wait_ge(s_g[k][g], (i + 1) * (16 * len([s for s in slots(g) if s])))
                    dst = take(i, ("group", k, g), part)
                    for n, s in enumerate(slots(g)):
                        for h in range(2):
                            at = (2 * n + h) * P
                            last = nc.tensor.transpose(dst[:, :].bitcast(bf16)[:, at:at + P], e16[:, k, s, h, :],
                                                       ident_b[:])
                    last.then_inc(s_tr, 1)

            def grams(i, k):
                wait_copied(pe, i, *[("small", u) for u in range(SU)], *[("group", k, g) for g in range(GROUPS)])
                for u in range(UNITS):
                    pe.wait_ge(s_unit[UNIT_BY[u]], i * UNITS + (k * UNITS // 2 + u // 2 + 1))
                    if u == 1:
                        wait_copied(pe, i - 1 + k, ("z", 1 - k))
                    for n in range(UG):
                        v = eT[:, k, SG * (UG * u + n):SG * (UG * u + n + 1), :]
                        per = UG // 2
                        col = n % per * SG * F
                        last = nc.tensor.matmul(gram[u % 2][:, n // per, col:col + SG * F],
                                                v.rearrange("p s f -> p (s f)"), v[:, :, 0:F],
                                                start=True, stop=True, skip_group_check=True)
                    last.then_inc(s_gram, 1)

            def z_transposes(i, k):
                pe.wait_ge(s_zc, i * 2 + (k + 1))
                for m in range(KT):
                    last = nc.tensor.transpose(z_bank[0:KP, m * P:(m + 1) * P], zc[:, k, m * KP:(m + 1) * KP], ident[:])
                last.then_inc(s_zp, 1)


            def layer1(i, u, samples=slice(0, NP), part=STEP):
                dst = take(i, ("h1", u), part)
                for v in range(2):
                    c = 2 * u + v
                    o = dst[:, v * NP:(v + 1) * NP][:, samples]
                    for m in range(KT):
                        nc.tensor.matmul(o, w1z[:, m, c * P:(c + 1) * P], zT[:, m, samples], start=m == 0, stop=False)
                    last = nc.tensor.matmul(o, w1r[:, c * P:(c + 1) * P], rT[:, samples], start=False, stop=True)
                last.then_inc(s_h1p, 1)

            def layer2(i, v, samples=slice(0, NP), part=STEP):
                dst = take(i, ("h2", v), part)
                for c in range(C1):
                    if v == 0 and c % 2 == 0:
                        wait_copied(pe, i, ("h1", c // 2))
                    last = nc.tensor.matmul(dst[:, samples], w2s[:, c, v * P:(v + 1) * P], h1[:, c, samples],
                                            start=c == 0, stop=c == C1 - 1)
                last.then_inc(s_h2p, 1)

            def layer3(i, samples=slice(0, NP), part=STEP):
                dst = take(i, ("y", 0), part)
                for c in range(C2):
                    wait_copied(pe, i, ("h2", c))
                    last = nc.tensor.matmul(dst[0:1, samples], w3s[:, c:c + 1], h2[:, c, samples],
                                            start=c == 0, stop=c == C2 - 1)
                last.then_inc(s_yp, 1)

            pe.wait_ge(s_ident, 1)
            pe.wait_ge(s_ident_b, 1)
            pe.wait_ge(s_pad, 1)
            transposes(0, 0, [0], FIRST)
            small_tables(0, [0], FIRST)
            transposes(0, 0, [1, 2, 3], FIRST)
            small_tables(0, [1], FIRST)
            small_tables(0, [2], FIRST)
            transposes(0, 0, [4, 5], FIRST)
            transposes(0, 1, [0, 1], FIRST)
            grams(0, 0)
            transposes(0, 1, [2, 3], FIRST)
            small_tables(1, [0], FIRST)
            transposes(0, 1, [4, 5], FIRST)

            def step(i, part):
                z_transposes(i, 0)
                grams(i, 1)
                transposes(i + 1, 0, [0, 1], part)
                small_tables(i + 1, [1], part)
                transposes(i + 1, 0, [2, 3], part)
                z_transposes(i, 1)
                small_tables(i + 1, [2], part)
                wait_copied(pe, i, ("z", 0), ("z", 1))
                pe.wait_ge(s_w, 16 * 6)
                layer1(i, 0, part=part)
                layer1(i, 1, part=part)
                transposes(i + 1, 0, [4, 5], part)
                layer2(i, 0, part=part)
                grams(i + 1, 0)
                transposes(i + 1, 1, [0, 1, 2], part)
                layer2(i, 1, part=part)
                transposes(i + 1, 1, [3], part)

            with pe.Fori(0, PAIRS - 2) as i:
                step(i, STEP)
                small_tables(i + 2, [0])
                transposes(i + 1, 1, [4, 5])
                layer3(i)
            step(PAIRS - 2, LAST)
            first, second = slice(0, P), slice(P, NP)
            transposes(PAIRS - 1, 1, [4, 5], LAST)
            layer3(PAIRS - 2, part=LAST)
            z_transposes(PAIRS - 1, 0)
            grams(PAIRS - 1, 1)
            wait_copied(pe, PAIRS - 1, ("z", 0))
            layer1(PAIRS - 1, 0, first, LAST)
            layer1(PAIRS - 1, 1, first, LAST)
            z_transposes(PAIRS - 1, 1)
            layer2(PAIRS - 1, 0, first, LAST)
            layer2(PAIRS - 1, 1, first, LAST)
            wait_copied(pe, PAIRS - 1, ("z", 1))
            layer1(PAIRS, 0, second, LAST)
            layer1(PAIRS, 1, second, LAST)
            layer3(PAIRS - 1, first, LAST)
            layer2(PAIRS, 0, second, LAST)
            layer2(PAIRS, 1, second, LAST)
            layer3(PAIRS, second, LAST)


        def copy_small(engine, copy, by, i, uses, first=False):
            for u in uses:
                if SMALL_BY[u] == by:
                    if not first:
                        engine.wait_ge(s_gram, i * (2 * UNITS))
                    engine.wait_ge(s_small, i * SU + (u + 1))
                    small_copy(copy, u).then_inc(s_copied["small", by], 1)

        def copy_groups(engine, copy, by, i, k, groups=range(GROUPS)):
            for g in groups:
                if GROUP_BY[g] == by:
                    if g == 0:
                        wait_copied(engine, i - 1, ("z", k))
                    engine.wait_ge(s_tr, i * (2 * GROUPS) + (k * GROUPS + g + 1))
                    group_copy(copy, k, g).then_inc(s_copied["group", by], 1)

        def copy_units(engine, copy, by, i, k, units=range(UNITS)):
            engine.wait_ge(s_z, i * 2 + (k + 1))
            for u in units:
                if UNIT_BY[u] == by:
                    engine.wait_ge(s_gram, i * (2 * UNITS) + (k * UNITS + u + 1))
                    for s in range(SG):
                        rows = slice(FP * s, FP * (s + 1))
                        src = gram[u % 2][rows, :, 0:UG // 2 * SG * F].rearrange("p h (g w) -> p h g w", w=SG * F)
                        dst = gr[rows, k, UG * u:UG * (u + 1), :].rearrange("p (h g) f -> p h g f", h=2)
                        last = copy(dst, src[:, :, :, s * F:(s + 1) * F])
                    last.then_inc(s_unit[by], 1)

        @block.scalar
        def _(act):
            act.sem_inc(s_copied["h1", A], 2)
            act.sem_inc(s_copied["h2", A], 2)
            act.sem_inc(s_unit[A], 1)

            def pack(i, k):
                act.wait_ge(s_z, i * 2 + (k + 3))
                nc.scalar.copy(zc[:, k, :].rearrange("p (f o) -> p f o", f=F), z_pairs(k)).then_inc(s_zc, 1)

            def relu1(i, u, samples=slice(0, NP)):
                act.wait_ge(s_w, 16 * 6)
                act.wait_ge(s_h1p, i * 2 + (u + 1))
                for v in range(2):
                    c = 2 * u + v
                    last = nc.scalar.activation(h1[:, c, samples], bank(("h1", u))[:, v * NP:(v + 1) * NP][:, samples],
                                                ACT.Relu, bias=b1s[:, c:c + 1])
                last.then_inc(s_copied["h1", A], 1)

            def relu2(i, v, samples=slice(0, NP)):
                act.wait_ge(s_h2p, i * C2 + (v + 1))
                nc.scalar.activation(h2[:, v, samples], bank(("h2", v))[:, samples], ACT.Relu,
                                     bias=b2s[:, v:v + 1]).then_inc(s_copied["h2", A], 1)

            copy = nc.scalar.copy
            copy_small(act, copy, A, 0, [0], first=True)
            copy_groups(act, copy, A, 0, 0, [1])
            copy_groups(act, copy, A, 0, 0, [2])
            copy_small(act, copy, A, 0, [2], first=True)
            copy_groups(act, copy, A, 0, 0, [4])
            copy_groups(act, copy, A, 0, 1, [1])
            copy_units(act, copy, A, 0, 0)
            copy_groups(act, copy, A, 0, 1, [2])
            pack(0, 0)
            copy_groups(act, copy, A, 0, 1, [4])

            def step(i):
                copy_units(act, copy, A, i, 1)
                copy_small(act, copy, A, i + 1, [0])
                copy_groups(act, copy, A, i + 1, 0, [1])
                pack(i, 1)
                copy_groups(act, copy, A, i + 1, 0, [2])
                copy_small(act, copy, A, i + 1, [2])
                relu1(i, 0)
                relu1(i, 1)
                copy_groups(act, copy, A, i + 1, 0, [4])
                relu2(i, 0)
                copy_units(act, copy, A, i + 1, 0)
                copy_groups(act, copy, A, i + 1, 1, [1, 2])
                pack(i + 1, 0)
                relu2(i, 1)
                copy_groups(act, copy, A, i + 1, 1, [4])

            with act.Fori(0, PAIRS - 2) as i:
                step(i)
            step(PAIRS - 2)
            first, second = slice(0, P), slice(P, NP)
            copy_units(act, copy, A, PAIRS - 1, 1)
            relu1(PAIRS - 1, 0, first)
            pack(PAIRS - 1, 1)
            relu1(PAIRS - 1, 1, first)
            relu2(PAIRS - 1, 0, first)
            relu2(PAIRS - 1, 1, first)
            relu1(PAIRS, 0, second)
            relu1(PAIRS, 1, second)
            relu2(PAIRS, 0, second)
            relu2(PAIRS, 1, second)

        @block.vector
        def _(dve):
            copy = nc.vector.tensor_copy
            dve.sem_inc(s_z, 2)
            dve.sem_inc(s_copied["z", V], 2)
            dve.sem_inc(s_copied["y", V], 1)
            dve.sem_inc(s_unit[V], 1)

            def narrow_ids(i):
                dve.wait_ge(s_ids_b, i * 16 + 16)
                copy(ids_h[:], ids_b[:]).then_inc(s_ids_h, 1)
                dve.wait_ge(s_ids_h, i + 1)

            def one_hot(chunks=range(SC)):
                for c in chunks:
                    last = nc.vector.tensor_scalar(onehot[:, c], ids_h[0:SP], row_of[:, c:c + 1], None, ALU.is_equal)
                if SC - 1 in chunks:
                    last.then_inc(s_onehot, 1)

            dve.wait_ge(s_ident, 1)
            copy(ident_b[:], ident[:]).then_inc(s_ident_b, 1)
            nc.vector.memset(eT[:, :, :, F:FP], 0.0).then_inc(s_pad, 1)
            dve.wait_ge(s_iota, 1)
            copy(row_of[:], row_of_i[:]).then_inc(s_row_of, 1)
            dve.wait_ge(s_row_of, 1)
            narrow_ids(0)
            one_hot()

            def less(j, part):
                if part:
                    dve.wait_ge(s_split[j], 1)
                    nc.vector.tensor_tensor(last_part[:, j], rest[:, j], parts[1][:, j], ALU.subtract).then_inc(s_split[j], 1)
                else:
                    dve.wait_ge(s_tab[j], 16)
                    nc.vector.tensor_tensor(rest[:, j], whole[:, j], parts[0][:, j], ALU.subtract).then_inc(s_split[j], 1)

            def gram_rows(i, k):
                for by in (A, V):
                    dve.wait_ge(s_unit[by], i * UNITS + ((k + 1) * UNITS // 2 + 1))
                nc.vector.transpose(z[:, k, :, 0:F].rearrange("p f g -> p g f"),
                                    gr[:, k].rearrange("p q g -> p g q"))
                nc.vector.transpose(z[:, k, :, F:W].rearrange("p f g -> p g f"),
                                    gr[:, k, :, 0:H].rearrange("p q g -> p g q")).then_inc(s_z, 1)

            def copy_pairs(i, k):
                dve.wait_ge(s_zp, i * 2 + (k + 1))
                src = z_bank[0:KP, 0:KT * P].rearrange("p (m s q) -> p m q s", m=KT, s=SG)
                dst = zT[:, :, k * P:(k + 1) * P].rearrange("p m (q s) -> p m q s", s=SG)
                copy(rT[:, k * P:(k + 1) * P], eT[:, k, :, 0])
                copy(dst, src).then_inc(s_copied["z", V], 1)

            def copy_y(i, at, samples=slice(0, NP)):
                dve.wait_ge(s_yp, i + 1)
                dst = y[:, bass.ds(at, samples.stop - samples.start)]
                copy(dst, bank(("y", 0))[0:1, samples]).then_inc(s_copied["y", V], 1)

            def next_one_hot(i, chunks=range(SC)):
                dve.wait_ge(s_small, i * SU + SU)
                one_hot(chunks)

            less(0, 0)
            less(1, 0)
            less(0, 1)
            less(1, 1)
            copy_groups(dve, copy, V, 0, 0, [0])
            less(2, 0)
            less(3, 0)
            less(2, 1)
            less(3, 1)
            less(4, 0)
            copy_groups(dve, copy, V, 0, 0, [3])
            less(4, 1)
            copy_small(dve, copy, V, 0, [1], first=True)
            copy_groups(dve, copy, V, 0, 0, [5])
            narrow_ids(1)
            copy_groups(dve, copy, V, 0, 1, [0])
            next_one_hot(0, range(SC // 2))
            copy_units(dve, copy, V, 0, 0, [1])
            one_hot(range(SC // 2, SC))
            copy_units(dve, copy, V, 0, 0, [3])
            gram_rows(0, 0)
            copy_groups(dve, copy, V, 0, 1, [3, 5])

            def step(i, more):
                copy_pairs(i, 0)
                copy_units(dve, copy, V, i, 1)
                gram_rows(i, 1)
                copy_groups(dve, copy, V, i + 1, 0, [0])
                copy_small(dve, copy, V, i + 1, [1])
                copy_groups(dve, copy, V, i + 1, 0, [3])
                copy_pairs(i, 1)
                if more:
                    narrow_ids(i + 2)
                    next_one_hot(i + 1)
                copy_groups(dve, copy, V, i + 1, 0, [5])
                copy_units(dve, copy, V, i + 1, 0)
                copy_groups(dve, copy, V, i + 1, 1, [0])
                gram_rows(i + 1, 0)
                copy_groups(dve, copy, V, i + 1, 1, [3])

            with dve.Fori(0, PAIRS - 2) as i:
                step(i, True)
                copy_groups(dve, copy, V, i + 1, 1, [5])
                copy_y(i, i * NP)
            step(PAIRS - 2, False)
            copy_groups(dve, copy, V, PAIRS - 1, 1, [5])
            copy_pairs(PAIRS - 1, 0)
            copy_units(dve, copy, V, PAIRS - 1, 1)
            gram_rows(PAIRS - 1, 1)
            copy_y(PAIRS - 2, (PAIRS - 2) * NP)
            copy_pairs(PAIRS - 1, 1)
            copy_y(PAIRS - 1, (TILES - 2) * P, slice(0, P))
            copy_y(PAIRS, (TILES - 1) * P, slice(P, NP))


SMALL = [0, 4, 7, 9, 16]


def kernel(**inputs):
    import numpy as np
    import concourse.bacc as bacc
    from concourse.bass_utils import run_bass_kernel_spmd

    F, H = 27, 13
    gathered = [t for t in range(F - 1) if t not in SMALL]
    feature = [0] + [1 + t for t in gathered] + [1 + t for t in SMALL]
    place = {pair: n for n, pair in enumerate(zip(*np.triu_indices(F, k=1)))}
    order = [place[tuple(sorted((feature[f], feature[(f + o) % F])))] for f in range(F) for o in range(1, H + 1)]
    w1 = np.asarray(inputs["W_top1"])
    ids = np.asarray(inputs["ids"])
    ids_small = ids[:, SMALL].T
    arrays = {"bottom": inputs["r_bottom_output"], "ids": ids[:, gathered], "ids_small": ids_small}
    for t in range(F - 1):
        arrays[f"table{t}"] = inputs[f"tbl_{t}"]
    arrays |= {"w1": np.concatenate([w1[order], w1[len(order):]]), "b1": inputs["b_top1"],
               "w2": inputs["W_top2"], "b2": inputs["b_top2"], "w3": inputs["W_top3"]}
    arrays = {name: np.ascontiguousarray(a) for name, a in arrays.items()}

    nc = bacc.Bacc("TRN2", target_bir_lowering=False, num_devices=1)
    ap = {name: nc.dram_tensor(name, a.shape, mybir.dt.from_np(a.dtype), kind="ExternalInput").ap()
          for name, a in arrays.items()}
    out = nc.dram_tensor("out", (arrays["bottom"].shape[0], 1), mybir.dt.float32, kind="ExternalOutput").ap()
    dlrm_tower(nc, ap["bottom"], ap["ids"], ap["ids_small"], [ap[f"table{t}"] for t in gathered],
               [ap[f"table{t}"] for t in SMALL], ap["w1"], ap["b1"], ap["w2"], ap["b2"], ap["w3"], out)
    r = run_bass_kernel_spmd(nc, [arrays], core_ids=[0])
    return r.results[0]["out"]
```
